# Optimizing a Trainium2 kernel written in Bass

```python
import numpy as np
import jax
import jax.numpy as jnp

def _softmax(x, axis=-1):
    return jax.nn.softmax(x, axis=axis)

def _gelu(x):
    return jax.nn.gelu(x, approximate=True)

def _silu(x):
    return jax.nn.silu(x)

def _sigmoid(x):
    return jax.nn.sigmoid(x)

def _layernorm(x, axis=-1, eps=1e-05):
    m = jnp.mean(x, axis=axis, keepdims=True)
    v = jnp.var(x, axis=axis, keepdims=True)
    return (x - m) / jnp.sqrt(v + eps)

def _scatter_add(tgt, idx, src, axis=0):
    return tgt.at[idx].add(src)

def _segment_sum(src, seg, n):
    return jax.ops.segment_sum(src, seg, n)
kernel_name = 'mk_adaln_ffn_d1_seqx_r8_e84202'

def setup_inputs(seed: int=0):
    np.random.seed(seed)
    _w = jnp.asarray

    def _rec_inputs():
        import jax
        import jax.numpy as jnp
        _rk = jax.random.key(seed)
        x = 7.22e-05 + 1 * jax.random.normal(jax.random.fold_in(_rk, 1), (32, 128, 128), jnp.float32)
        _lenS = 128 - jax.random.randint(jax.random.fold_in(_rk, 7), (32,), 0, max(1, 128 // 4) + 1, jnp.int32)
        _lenS2 = 128 - jax.random.randint(jax.random.fold_in(_rk, 8), (32,), 0, max(1, 128 // 4) + 1, jnp.int32)
        cond_512 = 0.0061147 + 1.02565 * jax.random.normal(jax.random.fold_in(_rk, 11), (32, 64), jnp.float32)
        return (x, cond_512)
    x, cond_512 = _rec_inputs()

    def _L0_cond_setup():
        import jax, jax.numpy as jnp
        import numpy as np
        import math
        HEAD_NUM = 16
        EPS = 1e-08

        def modulated_linear(x, s, aff_w, aff_b, w, b):
            style = s @ aff_w.T + aff_b
            w_mod = w[None, :, :] * style[:, None, :]
            demod = jax.lax.rsqrt(jnp.sum(w_mod * w_mod, axis=2) + EPS)
            w_mod = w_mod * demod[:, :, None]
            return jnp.einsum('bni,boi->bno', x, w_mod) + b
        key = jax.random.key(seed)
        ks = jax.random.split(key, 6)
        B, N, F, S = (8, 128, 128, 64)
        return {'x': jax.random.normal(ks[0], (B, N, F), dtype=jnp.float32), 's': jax.random.normal(ks[1], (B, S), dtype=jnp.float32), 'k_aff_w': jax.random.normal(ks[2], (F, S), dtype=jnp.float32) * 0.02, 'k_aff_b': jnp.ones((F,), dtype=jnp.float32), 'k_w': jax.random.normal(ks[3], (F, F), dtype=jnp.float32) * 0.02, 'k_b': jnp.zeros((F,), dtype=jnp.float32), 'o_aff_w': jax.random.normal(ks[4], (F, S), dtype=jnp.float32) * 0.02, 'o_aff_b': jnp.ones((F,), dtype=jnp.float32), 'o_w': jax.random.normal(ks[5], (F, F), dtype=jnp.float32) * 0.02, 'o_b': jnp.zeros((F,), dtype=jnp.float32)}
    _L0_cond_all = _L0_cond_setup()
    _L0_cond_in = {k: v for k, v in _L0_cond_all.items() if k in ('k_aff_w', 'k_aff_b', 'k_w', 'k_b', 'o_aff_w', 'o_aff_b', 'o_w', 'o_b')}
    del _L0_cond_all

    def _L0_ffn_setup():
        import jax, jax.numpy as jnp
        import numpy as np
        E = 8
        TOP_K = 2
        H = 128
        F = 512
        LN_EPS = 1e-12
        key = jax.random.key(seed)
        ks = jax.random.split(key, 9)
        s = lambda k, shape, scale: jax.random.normal(k, shape, dtype=jnp.float32) * scale
        return {'hidden_states': s(ks[0], (4, 256, H), 1.0), 'Wr': s(ks[1], (E, H), 0.02), 'br': jnp.zeros((E,), jnp.float32), 'W1': s(ks[2], (E, F, H), 0.02), 'b1': jnp.zeros((E, F), jnp.float32), 'W2': s(ks[3], (E, H, F), 0.02), 'b2': jnp.zeros((E, H), jnp.float32), 'ln_w': jnp.ones((H,), jnp.float32), 'ln_b': jnp.zeros((H,), jnp.float32)}
    _L0_ffn_all = _L0_ffn_setup()
    _L0_ffn_in = {k: v for k, v in _L0_ffn_all.items() if k in ('Wr', 'br', 'W1', 'b1', 'W2', 'b2', 'ln_w', 'ln_b')}
    del _L0_ffn_all
    return {'x': x, 'cond_512': cond_512, 'L0_cond_k_aff_w': _L0_cond_in['k_aff_w'], 'L0_cond_k_aff_b': _L0_cond_in['k_aff_b'], 'L0_cond_k_w': _L0_cond_in['k_w'], 'L0_cond_k_b': _L0_cond_in['k_b'], 'L0_cond_o_aff_w': _L0_cond_in['o_aff_w'], 'L0_cond_o_aff_b': _L0_cond_in['o_aff_b'], 'L0_cond_o_w': _L0_cond_in['o_w'], 'L0_cond_o_b': _L0_cond_in['o_b'], 'L0_ffn_Wr': _L0_ffn_in['Wr'], 'L0_ffn_br': _L0_ffn_in['br'], 'L0_ffn_W1': _L0_ffn_in['W1'], 'L0_ffn_b1': _L0_ffn_in['b1'], 'L0_ffn_W2': _L0_ffn_in['W2'], 'L0_ffn_b2': _L0_ffn_in['b2'], 'L0_ffn_ln_w': _L0_ffn_in['ln_w'], 'L0_ffn_ln_b': _L0_ffn_in['ln_b']}

def reference(x, cond_512, L0_cond_k_aff_w, L0_cond_k_aff_b, L0_cond_k_w, L0_cond_k_b, L0_cond_o_aff_w, L0_cond_o_aff_b, L0_cond_o_w, L0_cond_o_b, L0_ffn_Wr, L0_ffn_br, L0_ffn_W1, L0_ffn_b1, L0_ffn_W2, L0_ffn_b2, L0_ffn_ln_w, L0_ffn_ln_b):
    import jax
    import jax.numpy as jnp

    def _L0_cond_ref(x, s, k_aff_w, k_aff_b, k_w, k_b, o_aff_w, o_aff_b, o_w, o_b):
        import jax, jax.numpy as jnp
        import numpy as np
        import math
        HEAD_NUM = 16
        EPS = 1e-08

        def modulated_linear(x, s, aff_w, aff_b, w, b):
            style = s @ aff_w.T + aff_b
            w_mod = w[None, :, :] * style[:, None, :]
            demod = jax.lax.rsqrt(jnp.sum(w_mod * w_mod, axis=2) + EPS)
            w_mod = w_mod * demod[:, :, None]
            return jnp.einsum('bni,boi->bno', x, w_mod) + b
        B, N, F = x.shape
        H = HEAD_NUM
        D = F // H
        kx = modulated_linear(x, s, k_aff_w, k_aff_b, k_w, k_b)
        kx = kx.reshape(B, N, H, D)
        q = k = v = kx
        scores = jnp.einsum('bnhd,bnjd->bnhj', q, k) / math.sqrt(D)
        A = jax.nn.softmax(scores, axis=-1)
        out = jnp.einsum('bnhj,bnjd->bnhd', A, v).reshape(B, N, F)
        out = modulated_linear(out, s, o_aff_w, o_aff_b, o_w, o_b)
        return out

    def _L0_ffn_ref(hidden_states, Wr, br, W1, b1, W2, b2, ln_w, ln_b):
        import jax, jax.numpy as jnp
        import numpy as np
        E = 8
        TOP_K = 2
        H = 128
        F = 512
        LN_EPS = 1e-12
        bsz, seqlen, h = hidden_states.shape
        x = hidden_states.reshape(-1, h)
        logits = x @ Wr.T + br
        topk_vals, topk_idx = jax.lax.top_k(logits, TOP_K)
        topk_w = jax.nn.softmax(topk_vals, axis=-1)
        out = jnp.zeros_like(x)
        for e in range(E):
            cw = jnp.sum(topk_w * (topk_idx == e), axis=-1)
            y = jax.nn.gelu(x @ W1[e].T + b1[e], approximate=False) @ W2[e].T + b2[e]
            out = out + cw[:, None] * y
        z = out + x
        mu = jnp.mean(z, axis=-1, keepdims=True)
        var = jnp.mean(jnp.square(z - mu), axis=-1, keepdims=True)
        z = (z - mu) * jax.lax.rsqrt(var + LN_EPS) * ln_w + ln_b
        return z.reshape(bsz, seqlen, h)
    x = x + _L0_ffn_ref(_L0_cond_ref(x, cond_512, L0_cond_k_aff_w, L0_cond_k_aff_b, L0_cond_k_w, L0_cond_k_b, L0_cond_o_aff_w, L0_cond_o_aff_b, L0_cond_o_w, L0_cond_o_b), L0_ffn_Wr, L0_ffn_br, L0_ffn_W1, L0_ffn_b1, L0_ffn_W2, L0_ffn_b2, L0_ffn_ln_w, L0_ffn_ln_b)
    return x

_drawn_inputs = setup_inputs


def setup_inputs(seed=0):
    import zlib

    import numpy as np

    out = dict(_drawn_inputs(seed))
    spreads = {'L0_cond_k_aff_b': (1.0, 0.2),
     'L0_cond_k_b': (0.0, 0.1),
     'L0_cond_o_aff_b': (1.0, 0.2),
     'L0_cond_o_b': (0.0, 0.1),
     'L0_ffn_br': (0.0, 0.1),
     'L0_ffn_b1': (0.0, 0.454),
     'L0_ffn_b2': (0.0, 0.1),
     'L0_ffn_ln_w': (1.0, 0.2),
     'L0_ffn_ln_b': (0.0, 0.1)}
    factors = {}
    for name, (base, spread) in spreads.items():
        noise = np.random.default_rng([zlib.crc32(name.encode()), seed]).standard_normal(out[name].shape)
        drawn = base * np.exp(spread * noise) if base else spread * noise
        out[name] = jnp.asarray(drawn.astype(out[name].dtype))
    for name, factor in factors.items():
        out[name] = (out[name] * factor).astype(out[name].dtype)
    return out
```

```python
import math
from contextlib import ExitStack

import concourse.bass as bass
from concourse import mybir


class Step:

    def __init__(self, pair, k):
        self.c = pair * 2 + k
        self.u = k % 2
        self.use = pair + k // 2
        self.pair, self.k = pair, k

    def __add__(self, d):
        return Step(self.pair, self.k + d)


class Chain:

    def __init__(self, engine, sem, per_turn):
        self.engine, self.sem, self.per_turn = engine, sem, per_turn

    def turn(self, turn):
        self.base, self.n = turn * self.per_turn, 0

    def __call__(self, ins):
        self.n += 1
        ins.then_inc(self.sem, 1)
        self.engine.wait_ge(self.sem, self.base + self.n)

    def end(self):
        assert self.n == self.per_turn, self.n


def adaln_ffn(nc, x, cond, k_aff_w, k_aff_b, k_w, k_b, o_aff_w, o_aff_b, o_w, o_b, Wr, br, W1, b1, W2, b2,
              ln_w, ln_b, out):
    f32, u32 = mybir.dt.float32, mybir.dt.uint32
    ALU, ACT, AX = mybir.AluOpType, mybir.ActivationFunctionType, mybir.AxisListType

    B, N, F = x.shape
    S = cond.shape[1]
    E, FF = W1.shape[0], W1.shape[1]
    Q = FF // 128
    H = 16
    D = F // H
    J = 4
    C = B // J
    T = J * N
    R = H // 2 + 1
    PROBE_EPS, LN_EPS = 1e-8, 1e-12
    SCALE = 1.0 / math.sqrt(D)

    with ExitStack() as ctx:
        def sb(name, shape, dt=f32):
            return ctx.enter_context(nc.sbuf_tensor(name, shape, dt))

        def pb(name, shape=(128, 512), dt=f32):
            return ctx.enter_context(nc.psum_tensor(name, list(shape), dt))

        def sem(name):
            return ctx.enter_context(nc.semaphore(name))

        kaw, oaw = sb("kaw", [F, S]), sb("oaw", [F, S])
        cond_sb = sb("cond_sb", [B, S])
        kw, ow = sb("kw", [F, F]), sb("ow", [F, F])
        wr = sb("wr", [E, F])
        rows = sb("rows", [E * Q + 4, F])
        w1 = sb("w1", [128, E, Q, F])
        w2 = sb("w2", [F, E, FF])
        b2_sb = sb("b2_sb", [E, F])
        br_sb = sb("br_sb", [1, E])
        lnw, lnb = sb("lnw", [128, F]), sb("lnb", [128, F])
        ident = sb("ident", [128, 128])
        ones = sb("ones", [1, 128])
        iota_e = sb("iota_e", [128, E])
        kwT, owT = sb("kwT", [F, F]), sb("owT", [F, F])
        kwT2, owT2 = sb("kwT2", [F, F]), sb("owT2", [F, F])
        cols = sb("cols", [F, E * Q + 4])
        wrT = sb("wrT", [F, E])
        affT = sb("affT", [S, 2, F])
        condT = sb("condT", [S, B])
        style = sb("style", [F, 2, B])
        style2 = sb("style2", [F, 2, B])
        dsum = sb("dsum", [F, 2, B])
        dtmp = sb("dtmp", [F, 2, B])
        demod = sb("demod", [F, 2, B])
        w1T = sb("w1T", [F, E, FF])
        w2T = sb("w2T", [128, E, Q, F])
        xin = sb("xin", [128, 2, J, F])
        xT = sb("xT", [F, J, N])
        kT = sb("kT", [F, J, N])
        kk = sb("kk", [128, 2, J, 2, F])
        prod = sb("prod", [128, J, R, F])
        S2 = sb("S2", [128, J, R, 2, H])
        SF = sb("SF", [128, J, H, H])
        mx = sb("mx", [128, J, H])
        dif = sb("dif", [128, J, H, H])
        prob = sb("prob", [128, 2, J, H, H])
        rs = sb("rs", [128, J, H])
        rinv = sb("rinv", [128, J, H])
        av = sb("av", [128, J, H, F])
        oT = sb("oT", [F, J, N])
        zT = sb("zT", [F, 2, J, N])
        z = sb("z", [128, 2, J, F])
        lg = sb("lg", [128, J, E])
        top = sb("top", [128, J, 8])
        topi = sb("topi", [128, J, 8], u32)
        topf = sb("topf", [128, J, 8])
        gap = sb("gap", [128, J, 1])
        eg = sb("eg", [128, J, 1])
        w01 = sb("w01", [128, J, 2])
        cwa = sb("cwa", [128, J, E])
        cwb = sb("cwb", [128, J, E])
        cw = sb("cw", [128, J, E])
        cwT = sb("cwT", [E, J, N])
        h = sb("h", [128, 2, Q, T])
        acc = sb("acc", [128, J, F])
        mean = sb("mean", [128, J])
        cen = sb("cen", [128, J, F])
        sq = sb("sq", [128, J, F])
        var = sb("var", [128, J])
        std = sb("std", [128, J])
        y0 = sb("y0", [128, J])
        y1 = sb("y1", [128, J])
        ln1 = sb("ln1", [128, J, F])
        xres = sb("xres", [128, 2, J, F])
        fin = sb("fin", [128, 2, J, F])

        pX, pK, pO, pZ, pZt, pR = pb("pX"), pb("pK"), pb("pO"), pb("pZ"), pb("pZt"), pb("pR")
        pH = [pb("pH0"), pb("pH1")]
        pY = [pO, pZ]

        def tiles(p):
            return p[:, :].rearrange("p (j n) -> p j n", j=J)

        names = ["w_in", "w12_in", "const0", "const1", "wt_ps", "wt_ready", "style_ps", "style_ready", "dsum_ps",
                 "std_ready", "demod_ready", "wT_ps", "wT_ready", "setup_dve",
                 "xT_ps", "xT_ready", "kT_ps", "kT_ready", "k_ps", "kk_ready", "s_ready", "dup_ready", "sf_ready",
                 "dif_ready", "prob_exp", "norm_ready", "av_ready", "o_ps", "oT_ready", "z_ps", "zT_ready", "zt_ps",
                 "z_ready", "lg_ps", "gap_ready", "eg_ready", "cw_ready", "cwT_ps", "cwT_ready", "bias_ps", "h_ps",
                 "h_ready", "y_ps", "y_used", "cen_ready", "sq_ready", "ve_ready", "sd_ready", "cy_ready", "ln_ready",
                 "lnp", "att_chain", "tail_chain", "acc_start"]
        s = {n: sem(n) for n in names}
        x_in = [sem("x_in0"), sem("x_in1")]
        xres_in = [sem("xres_in0"), sem("xres_in1")]
        out_done = [sem("out_done0"), sem("out_done1")]

        def x_of(st):
            return x[bass.ds(st.c * J, J)].rearrange("b n f -> n b f")

        def out_of(st):
            return out[bass.ds(st.c * J, J)].rearrange("b n f -> n b f")

        def turns(engine, body):
            body(Step(0, 0), True, False)
            with engine.Fori(0, (C - 2) // 2) as pair:
                body(Step(pair, 1), False, False)
                body(Step(pair, 2), False, False)
            body(Step((C - 2) // 2, 1), False, True)

        LAST = Step((C - 2) // 2, 1)
        W_SMALL = 12 + 4

        with nc.Block() as block:
            @block.sync
            def _(sp):
                def load(dst, src, done):
                    sp.dma_start(dst, src).then_inc(done, 16)

                load(kw[:, :], k_w, s["w_in"])
                load(ow[:, :], o_w, s["w_in"])
                load(kaw[:, :], k_aff_w, s["w_in"])
                load(oaw[:, :], o_aff_w, s["w_in"])
                load(cond_sb[:, :], cond, s["w_in"])
                load(wr[:, :], Wr, s["w_in"])
                load(rows[0:E * Q, :], b1.rearrange("e (q f) -> (e q) f", q=Q), s["w_in"])
                for n, v in enumerate((k_aff_b, k_b, o_aff_b, o_b)):
                    load(rows[E * Q + n:E * Q + n + 1, :], v.unsqueeze(0), s["w_in"])
                load(b2_sb[:, :], b2, s["w_in"])
                load(br_sb[:, :], br.unsqueeze(0), s["w_in"])
                load(lnw[:, :], ln_w.unsqueeze(0).broadcast_to([128, F]), s["w_in"])
                load(lnb[:, :], ln_b.unsqueeze(0).broadcast_to([128, F]), s["w_in"])
                load(xin[:, 0], x_of(Step(0, 0)), x_in[0])
                load(w1[:, :, :, :], W1.rearrange("e (q f) h -> f e q h", q=Q), s["w12_in"])
                load(w2[:, :, :], W2.rearrange("e h f -> h e f"), s["w12_in"])

                def step(st, first, last):
                    if not last:
                        nx = st + 1
                        if not first:
                            sp.wait_ge(s["xT_ps"], st.c)
                        load(xin[:, nx.u], x_of(nx), x_in[nx.u])
                    if not first:
                        tail(st + -1)

                def tail(st):
                    sp.wait_ge(s["cy_ready"], st.c + 1)
                    load(xres[:, st.u], x_of(st), xres_in[st.u])
                    sp.wait_ge(s["ln_ready"], st.c + 2)
                    sp.dma_start(out_of(st), fin[:, st.u]).then_inc(out_done[st.u], 16)

                turns(sp, step)
                tail(LAST)
                for u in range(2):
                    sp.wait_ge(out_done[u], 16 * (C // 2) + 16)

            @block.gpsimd
            def _(pool):
                nc.gpsimd.memset(ident[:, :], 0.0).then_inc(s["const0"], 1)
                nc.gpsimd.memset(ones[:, :], 1.0)
                nc.gpsimd.iota(iota_e[:, :], [[1, E]], base=0, channel_multiplier=0,
                               allow_small_or_imprecise_dtypes=True)
                pool.wait_ge(s["const0"], 1)
                nc.gpsimd.affine_select(out=ident[:, :], in_=ident[:, :], compare_op=ALU.not_equal, fill=1.0, base=0,
                                        pattern=[[-1, 128]], channel_multiplier=1).then_inc(s["const1"], 1)

                pool.wait_ge(s["w_in"], 16 * 15)
                chain = Chain(pool, s["lnp"], 2)
                pool.sem_inc(s["cy_ready"], 1)
                pool.sem_inc(s["ln_ready"], 1)
                for u in range(2):
                    pool.sem_inc(out_done[u], 16)

                def tail(st):
                    chain.turn(st.c)
                    pool.wait_ge(s["cen_ready"], 2 * st.c + 2)
                    pool.wait_ge(out_done[st.u], st.use * 16 + 16)
                    chain(nc.gpsimd.tensor_tensor(out=ln1[:, :, :], in0=cen[:, :, :],
                                                  in1=lnw[:, :].unsqueeze(1).broadcast_to([128, J, F]), op=ALU.mult))
                    chain(nc.gpsimd.tensor_tensor(out=ln1[:, :, :], in0=ln1[:, :, :],
                                                  in1=lnb[:, :].unsqueeze(1).broadcast_to([128, J, F]), op=ALU.add))
                    pool.wait_ge(xres_in[st.u], st.use * 16 + 16)
                    nc.gpsimd.tensor_tensor(out=fin[:, st.u], in0=ln1[:, :, :], in1=xres[:, st.u],
                                            op=ALU.add).then_inc(s["ln_ready"], 1)
                    pool.wait_ge(s["ln_ready"], st.c + 2)
                    pool.sem_inc(s["cy_ready"], 1)
                    chain.end()

                def step(st, first, last):
                    if not first:
                        tail(st + -1)

                turns(pool, step)
                tail(LAST)

            @block.scalar
            def _(act):
                COPY = ACT.Identity
                act.wait_ge(s["style_ready"], 2)
                nc.scalar.activation(dtmp[:, :, :], dsum[:, :, :], ACT.Sqrt).then_inc(s["std_ready"], 1)
                for e in range(E):
                    for n, dst in enumerate((w1T[:, e], w2T[:, e].rearrange("f q h -> f (q h)"))):
                        act.wait_ge(s["wT_ps"], 2 * e + n + 1)
                        nc.scalar.copy(dst, pH[n][:, :]).then_inc(s["wT_ready"], 1)

                def per_batch(st, dst, src, scales, which, bias, done):
                    for j in range(J):
                        col = scales[:, which, bass.ds(st.c * J + j, 1)]
                        last = nc.scalar.activation(dst[:, j], src[:, j], COPY, scale=col, bias=bias)
                    last.then_inc(done, 1)

                def project_a(st):
                    act.wait_ge(s["xT_ps"], st.c + 1)
                    per_batch(st, xT, tiles(pX), style, 0, 0.0, s["xT_ready"])
                    act.wait_ge(s["kT_ps"], st.c + 1)
                    per_batch(st, kT, tiles(pK), demod, 0, cols[:, E * Q + 1:E * Q + 2], s["kT_ready"])

                def project_b(st):
                    act.wait_ge(s["k_ps"], st.c + 1)
                    act.wait_ge(s["av_ready"], (st.c + -1) * J)
                    nc.scalar.copy(kk[:, st.u], tiles(pX).unsqueeze(2).broadcast_to([128, J, 2, F])
                                   ).then_inc(s["kk_ready"], 1)

                def project_out(st):
                    act.wait_ge(s["o_ps"], J * st.c + 2 * J)
                    per_batch(st, oT, tiles(pO), style, 1, 0.0, s["oT_ready"])
                    act.wait_ge(s["z_ps"], st.c + 1)
                    per_batch(st, zT[:, st.u], tiles(pZ), demod, 1, cols[:, E * Q + 3:E * Q + 4], s["zT_ready"])
                    act.wait_ge(s["zt_ps"], st.c + 1)
                    nc.scalar.copy(z[:, st.u], tiles(pZt)).then_inc(s["z_ready"], 1)

                def ffn(st):
                    act.wait_ge(s["gap_ready"], st.c + 1)
                    nc.scalar.activation(eg[:, :, :], gap[:, :, :], ACT.Exp).then_inc(s["eg_ready"], 1)
                    for e in range(E):
                        for q in range(Q):
                            n = e * Q + q
                            act.wait_ge(s["h_ps"], st.c * (E * Q) + n + 1)
                            if q == 0:
                                act.wait_ge(s["y_ps"], st.c * E + e + 1)
                            nc.scalar.activation(h[:, e % 2, q], pH[q % 2][:, :], ACT.Gelu,
                                                 bias=cols[:, n:n + 1]).then_inc(s["h_ready"], 1)
                        if e == 0:
                            act.wait_ge(s["cwT_ps"], st.c + 1)
                            nc.scalar.copy(cwT[:, :, :], tiles(pR)[0:E]).then_inc(s["cwT_ready"], 1)
                    act.wait_ge(s["cen_ready"], 2 * st.c + 1)
                    for j in range(J):
                        last = nc.scalar.activation(sq[:, j], cen[:, j], ACT.Square, accum_out=var[:, j:j + 1])
                    last.then_inc(s["sq_ready"], 1)
                    act.wait_ge(s["ve_ready"], st.c + 1)
                    nc.scalar.activation(std[:, :], var[:, :], ACT.Sqrt).then_inc(s["sd_ready"], 1)

                def step(st, first, last):
                    if not last:
                        project_a(st + 1)
                    act.wait_ge(s["s_ready"], st.c + 1)
                    nc.scalar.copy(S2[:, :, 1:R, 1], S2[:, :, 1:R, 0]).then_inc(s["dup_ready"], 1)
                    nc.scalar.copy(SF[:, :, 0:R], S2[:, :, :, 0])
                    act.wait_ge(s["dup_ready"], st.c + 1)
                    row = list(S2[:, :, :, :, :].ap[0])
                    for j in range(J):
                        src = bass.AP(tensor=S2[:, :, :, :, :].tensor,
                                      offset=S2[:, j].offset + (H - R) * 2 * H + R,
                                      ap=[row, [1 - 2 * H, H - R], [1, H]])
                        lastc = nc.scalar.copy(SF[:, j, R:H], src)
                    lastc.then_inc(s["sf_ready"], 1)
                    act.wait_ge(s["dif_ready"], st.c + 1)
                    nc.scalar.activation(prob[:, st.u], dif[:, :, :, :], ACT.Exp, scale=SCALE
                                         ).then_inc(s["prob_exp"], 1)
                    if not last:
                        project_b(st + 1)
                    if not first:
                        project_out(st + -1)
                        ffn(st + -1)

                act.sem_inc(s["h_ready"], 2)
                act.sem_inc(s["cwT_ready"], 1)
                project_a(Step(0, 0))
                act.wait_ge(s["k_ps"], 1)
                nc.scalar.copy(kk[:, 0], tiles(pX).unsqueeze(2).broadcast_to([128, J, 2, F])).then_inc(s["kk_ready"], 1)
                turns(act, step)
                project_out(LAST)
                ffn(LAST)

            @block.vector
            def _(dve):
                V = nc.vector
                setup = Chain(dve, s["setup_dve"], 7)
                setup.turn(0)
                dve.wait_ge(s["wt_ps"], 1)
                V.tensor_copy(kwT[:, :], pX[:, 0:128])
                V.tensor_copy(owT[:, :], pX[:, 128:256])
                V.tensor_copy(cols[:, :], pX[:, 256:256 + E * Q + 4])
                V.tensor_copy(wrT[:, :], pX[:, 320:320 + E])
                V.tensor_copy(affT[:, :, :], pK[0:S, 0:256].rearrange("s (a f) -> s a f", a=2))
                V.tensor_copy(condT[:, :], pK[0:S, 256:256 + B]).then_inc(s["wt_ready"], 1)
                dve.wait_ge(s["wt_ready"], 1)
                V.tensor_tensor(out=kwT2[:, :], in0=kwT[:, :], in1=kwT[:, :], op=ALU.mult)
                V.tensor_tensor(out=owT2[:, :], in0=owT[:, :], in1=owT[:, :], op=ALU.mult)
                dve.wait_ge(s["style_ps"], 1)
                setup(V.tensor_tensor(out=style[:, 0], in0=pO[:, 0:B],
                                      in1=cols[:, E * Q:E * Q + 1].broadcast_to([F, B]), op=ALU.add))
                setup(V.tensor_tensor(out=style[:, 1], in0=pO[:, B:2 * B],
                                      in1=cols[:, E * Q + 2:E * Q + 3].broadcast_to([F, B]), op=ALU.add))
                V.tensor_tensor(out=style2[:, :, :], in0=style[:, :, :], in1=style[:, :, :], op=ALU.mult
                                ).then_inc(s["style_ready"], 1)
                dve.wait_ge(s["dsum_ps"], 1)
                V.tensor_scalar(out=dsum[:, :, :], in0=pZ[:, 0:2 * B].rearrange("p (a b) -> p a b", a=2),
                                scalar1=PROBE_EPS, scalar2=None, op0=ALU.add).then_inc(s["style_ready"], 1)
                dve.wait_ge(s["std_ready"], 1)

                def rsqrt(link, out_, v, sd, t):
                    link(V.reciprocal(sd, sd))
                    link(V.tensor_tensor(out=t, in0=sd, in1=v, op=ALU.mult))
                    link(V.tensor_tensor(out=t, in0=t, in1=sd, op=ALU.mult))
                    link(V.tensor_scalar(out=t, in0=t, scalar1=-0.5, scalar2=1.5, op0=ALU.mult, op1=ALU.add))
                    link(V.tensor_tensor(out=out_, in0=t, in1=sd, op=ALU.mult))

                rsqrt(setup, demod[:, :, :], dsum[:, :, :], dtmp[:, :, :], style2[:, :, :])
                dve.sem_inc(s["demod_ready"], 1)
                dve.sem_inc(s["acc_start"], 2)
                dve.sem_inc(s["y_used"], 1)

                att = Chain(dve, s["att_chain"], 4)
                tail_chain = Chain(dve, s["tail_chain"], 19 + E)

                def window(half, j0, nj, dist):
                    full = kk[:, :, :, :, :]
                    return bass.AP(tensor=full.tensor, offset=kk[:, half, j0].offset,
                                   ap=[list(full.ap[0]), [2 * F, nj], [D, dist], [1, F]])

                def attend(st, j):
                    dve.wait_ge(s["o_ps"], J * st.c + j + 1)
                    p = prob[:, st.u, j].unsqueeze(3).broadcast_to([128, H, H, D])
                    v = window(st.u, j, 1, H)
                    v = bass.AP(tensor=v.tensor, offset=v.offset, ap=[list(v.ap[0]), [D, H], [D, H], [1, D]])
                    V.tensor_tensor(out=av[:, j].rearrange("p s (h d) -> p s h d", d=D), in0=p, in1=v, op=ALU.mult
                                    ).then_inc(s["av_ready"], 1)

                def tail(st):
                    link = tail_chain
                    link.turn(st.c)
                    dve.wait_ge(s["lg_ps"], st.c + 1)
                    dve.wait_ge(s["z_ready"], st.c + 1)
                    link(V.tensor_copy(lg[:, :, :], pR[:, 0:J * E].rearrange("p (j e) -> p j e", e=E)))
                    V.tensor_copy(acc[:, :, :], z[:, st.u])
                    for j in range(J):
                        last = V.max(out=top[:, j], in_=lg[:, j])
                    link(last)
                    V.tensor_tensor(out=gap[:, :, :], in0=top[:, :, 1:2], in1=top[:, :, 0:1], op=ALU.subtract
                                    ).then_inc(s["gap_ready"], 1)
                    for j in range(J):
                        last = V.max_index(out=topi[:, j], in_max=top[:, j], in_values=lg[:, j])
                    link(last)
                    link(V.tensor_copy(topf[:, :, :], topi[:, :, :]))
                    bc = [128, J, E]
                    iot = iota_e[:, :].unsqueeze(1).broadcast_to(bc)
                    link(V.tensor_tensor(out=cwa[:, :, :], in0=topf[:, :, 0:1].broadcast_to(bc), in1=iot,
                                         op=ALU.is_equal))
                    link(V.tensor_tensor(out=cwb[:, :, :], in0=topf[:, :, 1:2].broadcast_to(bc), in1=iot,
                                         op=ALU.is_equal))
                    dve.wait_ge(s["eg_ready"], st.c + 1)
                    link(V.tensor_scalar(out=gap[:, :, :], in0=eg[:, :, :], scalar1=1.0, scalar2=None, op0=ALU.add))
                    link(V.reciprocal(w01[:, :, 0:1], gap[:, :, :]))
                    link(V.tensor_tensor(out=w01[:, :, 1:2], in0=eg[:, :, :], in1=w01[:, :, 0:1], op=ALU.mult))
                    V.tensor_tensor(out=cwa[:, :, :], in0=cwa[:, :, :], in1=w01[:, :, 0:1].broadcast_to(bc),
                                    op=ALU.mult)
                    link(V.tensor_tensor(out=cwb[:, :, :], in0=cwb[:, :, :], in1=w01[:, :, 1:2].broadcast_to(bc),
                                         op=ALU.mult))
                    link(V.tensor_tensor(out=cw[:, :, :], in0=cwa[:, :, :], in1=cwb[:, :, :], op=ALU.add))
                    dve.sem_inc(s["cw_ready"], 1)
                    dve.wait_ge(s["bias_ps"], st.c + 1)
                    link(V.tensor_tensor(out=acc[:, :, :], in0=acc[:, :, :], in1=tiles(pK), op=ALU.add))
                    dve.sem_inc(s["acc_start"], 1)
                    for e in range(E):
                        dve.wait_ge(s["y_ps"], st.c * E + e + 3)
                        for j in range(J):
                            last = V.scalar_tensor_tensor(out=acc[:, j], in0=tiles(pY[e % 2])[:, j],
                                                          scalar=cw[:, j, e:e + 1], in1=acc[:, j], op0=ALU.mult,
                                                          op1=ALU.add)
                        link(last)
                        dve.sem_inc(s["y_used"], 1)
                    link(V.tensor_reduce(out=mean[:, :], in_=acc[:, :, :], axis=AX.X, op=ALU.add))
                    link(V.tensor_scalar(out=mean[:, :], in0=mean[:, :], scalar1=1.0 / F, scalar2=None, op0=ALU.mult))
                    dve.wait_ge(s["ln_ready"], st.c + 1)
                    V.tensor_tensor(out=cen[:, :, :], in0=acc[:, :, :],
                                    in1=mean[:, :].unsqueeze(2).broadcast_to([128, J, F]), op=ALU.subtract
                                    ).then_inc(s["cen_ready"], 1)
                    dve.wait_ge(s["sq_ready"], st.c + 1)
                    V.tensor_scalar(out=var[:, :], in0=var[:, :], scalar1=1.0 / F, scalar2=LN_EPS, op0=ALU.mult,
                                    op1=ALU.add).then_inc(s["ve_ready"], 1)
                    dve.wait_ge(s["sd_ready"], st.c + 1)
                    rsqrt(link, y1[:, :], var[:, :], std[:, :], y0[:, :])
                    V.tensor_tensor(out=cen[:, :, :], in0=cen[:, :, :],
                                    in1=y1[:, :].unsqueeze(2).broadcast_to([128, J, F]), op=ALU.mult
                                    ).then_inc(s["cen_ready"], 1)
                    link.end()

                def step(st, first, last):
                    att.turn(st.c)
                    dve.wait_ge(s["kk_ready"], st.c + 1)
                    att(V.tensor_tensor(out=prod[:, :, :, :], in0=kk[:, st.u, :, 0:1].broadcast_to([128, J, R, F]),
                                        in1=window(st.u, 0, J, R), op=ALU.mult))
                    V.tensor_reduce(out=S2[:, :, :, 0],
                                    in_=prod[:, :, :, :].rearrange("p j r (h d) -> p j r h d", d=D), axis=AX.X,
                                    op=ALU.add).then_inc(s["s_ready"], 1)
                    if not first:
                        attend(st + -1, 0)
                        attend(st + -1, 1)
                    dve.wait_ge(s["sf_ready"], st.c + 1)
                    att(V.tensor_reduce(out=mx[:, :, :], in_=SF[:, :, :, :].rearrange("p j s h -> p j h s"),
                                        axis=AX.X, op=ALU.max))
                    V.tensor_tensor(out=dif[:, :, :, :], in0=SF[:, :, :, :],
                                    in1=mx[:, :, :].unsqueeze(2).broadcast_to([128, J, H, H]), op=ALU.subtract
                                    ).then_inc(s["dif_ready"], 1)
                    if not first:
                        attend(st + -1, 2)
                        attend(st + -1, 3)
                    dve.wait_ge(s["prob_exp"], st.c + 1)
                    p = prob[:, st.u]
                    att(V.tensor_reduce(out=rs[:, :, :], in_=p.rearrange("p j s h -> p j h s"), axis=AX.X,
                                        op=ALU.add))
                    att(V.reciprocal(rinv[:, :, :], rs[:, :, :]))
                    V.tensor_tensor(out=p, in0=p, in1=rinv[:, :, :].unsqueeze(2).broadcast_to([128, J, H, H]),
                                    op=ALU.mult).then_inc(s["norm_ready"], 1)
                    att.end()
                    dve.wait_ge(s["norm_ready"], st.c + 1)
                    if not first:
                        tail(st + -1)

                turns(dve, step)
                for j in range(J):
                    attend(LAST, j)
                tail(LAST)

            @block.tensor
            def _(pe):
                PE = nc.tensor

                def transpose(dst, src, n=128):
                    return PE.transpose(dst, src, ident[0:n, 0:n])

                pe.wait_ge(s["const1"], 1)
                pe.wait_ge(s["w_in"], 16 * 15)
                transpose(pX[:, 0:128], kw[:, :])
                transpose(pX[:, 128:256], ow[:, :])
                transpose(pX[:, 256:256 + E * Q + 4], rows[:, :], E * Q + 4)
                transpose(pX[:, 320:320 + E], wr[:, :], E)
                transpose(pK[0:S, 0:128], kaw[:, :])
                transpose(pK[0:S, 128:256], oaw[:, :])
                transpose(pK[0:S, 256:256 + B], cond_sb[:, :], B).then_inc(s["wt_ps"], 1)
                pe.wait_ge(s["wt_ready"], 1)
                PE.matmul(pO[:, 0:B], affT[:, 0], condT[:, :], start=True, stop=True)
                PE.matmul(pO[:, B:2 * B], affT[:, 1], condT[:, :], start=True, stop=True).then_inc(s["style_ps"], 1)
                pe.wait_ge(s["style_ready"], 1)
                PE.matmul(pZ[:, 0:B], kwT2[:, :], style2[:, 0], start=True, stop=True)
                PE.matmul(pZ[:, B:2 * B], owT2[:, :], style2[:, 1], start=True, stop=True).then_inc(s["dsum_ps"], 1)
                pe.wait_ge(s["w12_in"], 32)
                for e in range(E):
                    if e:
                        pe.wait_ge(s["wT_ready"], 2 * e - 1)
                    for q in range(Q):
                        last = transpose(pH[0][:, 128 * q:128 * q + 128], w1[:, e, q])
                    last.then_inc(s["wT_ps"], 1)
                    if e:
                        pe.wait_ge(s["wT_ready"], 2 * e)
                    for q in range(Q):
                        last = transpose(pH[1][:, 128 * q:128 * q + 128], w2[:, e, 128 * q:128 * q + 128])
                    last.then_inc(s["wT_ps"], 1)
                pe.wait_ge(s["demod_ready"], 1)

                def project(st):
                    pe.wait_ge(x_in[st.u], st.use * 16 + 16)
                    pe.wait_ge(s["kk_ready"], st.c)
                    for j in range(J):
                        last = transpose(tiles(pX)[:, j], xin[:, st.u, j])
                    last.then_inc(s["xT_ps"], 1)
                    pe.wait_ge(s["xT_ready"], st.c + 1)
                    pe.wait_ge(s["acc_start"], st.c)
                    PE.matmul(pK[:, :], kwT[:, :], xT[:, :, :].rearrange("p j n -> p (j n)"), start=True, stop=True
                              ).then_inc(s["kT_ps"], 1)
                    pe.wait_ge(s["kT_ready"], st.c + 1)
                    for j in range(J):
                        last = transpose(tiles(pX)[:, j], kT[:, j])
                    last.then_inc(s["k_ps"], 1)

                def project_out(st):
                    for j in range(J):
                        pe.wait_ge(s["av_ready"], J * st.c + j + 1)
                        if j == 0:
                            pe.wait_ge(s["y_used"], E * st.c + 1)
                        for d in range(H):
                            last = PE.matmul(tiles(pO)[:, j], av[:, j, d], ident[:, :], start=d == 0,
                                             stop=d == H - 1, is_transpose=True)
                        last.then_inc(s["o_ps"], 1)
                    pe.wait_ge(s["oT_ready"], st.c + 1)
                    PE.matmul(pZ[:, :], owT[:, :], oT[:, :, :].rearrange("p j n -> p (j n)"), start=True, stop=True
                              ).then_inc(s["z_ps"], 1)
                    pe.wait_ge(s["zT_ready"], st.c + 1)
                    for j in range(J):
                        last = transpose(tiles(pZt)[:, j], zT[:, st.u, j])
                    last.then_inc(s["zt_ps"], 1)
                    pe.wait_ge(s["cwT_ready"], st.c + 1)
                    for j in range(J):
                        o = pR[:, j * E:j * E + E]
                        PE.matmul(o, zT[:, st.u, j], wrT[:, :], start=True, stop=False)
                        last = PE.matmul(o, ones[:, :], br_sb[:, :], start=False, stop=True)
                    last.then_inc(s["lg_ps"], 1)

                def ffn(st):
                    def up(e):
                        for q in range(Q):
                            n = e * Q + q
                            pe.wait_ge(s["h_ready"], st.c * (E * Q) + n + 1)
                            PE.matmul(pH[q % 2][:, :], w1T[:, e, 128 * q:128 * q + 128],
                                      zT[:, st.u].rearrange("p j n -> p (j n)"), start=True, stop=True
                                      ).then_inc(s["h_ps"], 1)

                    up(0)
                    pe.wait_ge(s["cw_ready"], st.c + 1)
                    for j in range(J):
                        last = transpose(tiles(pR)[0:E, j], cw[:, j])
                    last.then_inc(s["cwT_ps"], 1)
                    pe.wait_ge(s["cwT_ready"], st.c + 2)
                    for j in range(J):
                        last = PE.matmul(tiles(pK)[:, j], cwT[:, j], b2_sb[:, :], start=True, stop=True)
                    last.then_inc(s["bias_ps"], 1)
                    for e in range(E):
                        if e + 1 < E:
                            up(e + 1)
                        pe.wait_ge(s["h_ready"], st.c * (E * Q) + (e * Q + Q + 2))
                        if e >= 2:
                            pe.wait_ge(s["y_used"], st.c * E + e)
                        for j in range(J):
                            for q in range(Q):
                                last = PE.matmul(tiles(pY[e % 2])[:, j], h[:, e % 2, q, N * j:N * j + N],
                                                 w2T[:, e, q], start=q == 0, stop=q == Q - 1)
                        last.then_inc(s["y_ps"], 1)

                def step(st, first, last):
                    if not last:
                        project(st + 1)
                    if not first:
                        project_out(st + -1)
                        ffn(st + -1)

                pe.sem_inc(s["y_ps"], 2)
                pe.sem_inc(s["o_ps"], J)
                project(Step(0, 0))
                turns(pe, step)
                project_out(LAST)
                ffn(LAST)


_INS = ['x', 'cond_512', 'L0_cond_k_aff_w', 'L0_cond_k_aff_b', 'L0_cond_k_w', 'L0_cond_k_b', 'L0_cond_o_aff_w',
        'L0_cond_o_aff_b', 'L0_cond_o_w', 'L0_cond_o_b', 'L0_ffn_Wr', 'L0_ffn_br', 'L0_ffn_W1', 'L0_ffn_b1',
        'L0_ffn_W2', 'L0_ffn_b2', 'L0_ffn_ln_w', 'L0_ffn_ln_b']


def kernel(**inputs):
    import numpy as _np
    import concourse.bacc as _bacc
    from concourse import mybir as _mybir
    from concourse.bass_utils import run_bass_kernel_spmd as _run

    nc = _bacc.Bacc("TRN2", target_bir_lowering=False, num_devices=1)
    arrays, args = {}, []
    for name in _INS:
        a = _np.ascontiguousarray(inputs[name])
        arrays[f"in_{name}_dram"] = a
        args.append(nc.dram_tensor(f"in_{name}_dram", a.shape, _mybir.dt.from_np(a.dtype), kind="ExternalInput").ap())
    y = nc.dram_tensor("out_dram", inputs['x'].shape, _mybir.dt.float32, kind="ExternalOutput").ap()
    adaln_ffn(nc, *args, y)
    r = _run(nc, [arrays], core_ids=[0])
    return r.results[0]["out_dram"]
```

```python
import math
from contextlib import ExitStack

import concourse.bass as bass
from concourse import mybir


class Chain:

    def __init__(self, engine, sem):
        self.engine, self.sem, self.n = engine, sem, 0

    def __call__(self, ins):
        self.n += 1
        ins.then_inc(self.sem, 1)
        self.engine.wait_ge(self.sem, self.n)


def adaln_ffn(nc, x, cond, k_aff_w, k_aff_b, k_w, k_b, o_aff_w, o_aff_b, o_w, o_b, Wr, br, W1, b1, W2, b2,
              ln_w, ln_b, out):
    f32, i32, u32, bf16 = mybir.dt.float32, mybir.dt.int32, mybir.dt.uint32, mybir.dt.bfloat16
    ALU, ACT, AX = mybir.AluOpType, mybir.ActivationFunctionType, mybir.AxisListType

    B, N, F = x.shape
    S = cond.shape[1]
    E, FF = W1.shape[0], W1.shape[1]
    Q = FF // 128
    H = 16
    D = F // H
    J = 4
    C = B // J
    R = H // 2 + 1
    GC = 2
    G = C // GC
    GT = GC * J
    TOP = 2
    K = TOP * GT + E - 1
    TURN = 12
    LAG = 8
    NB = 4
    LOADS = (4, K - 4)
    STORES = (8, 8, K - 16)
    DEMOD_EPS, LN_EPS = 1e-8, 1e-12
    SCALE = 1.0 / math.sqrt(D)

    xs = nc.dram_tensor("xs", (K * 128, F), f32, kind="Internal").ap()
    ys = nc.dram_tensor("ys", (K * 128, F), f32, kind="Internal").ap()
    w1s = nc.dram_tensor("w1s", (E * F, FF), f32, kind="Internal").ap()

    with ExitStack() as ctx:
        def sb(name, shape, dt=f32):
            return ctx.enter_context(nc.sbuf_tensor(name, shape, dt))

        def pb(name):
            return ctx.enter_context(nc.psum_tensor(name, [128, 512], f32))

        def sem(name):
            return ctx.enter_context(nc.semaphore(name))

        cond_sb, wr = sb("cond_sb", [B, S]), sb("wr", [E, F])
        rows = sb("rows", [4, F])
        br_sb = sb("br_sb", [1, E])
        lnw, lnb = sb("lnw", [128, F]), sb("lnb", [128, F])
        ident, ones = sb("ident", [128, 128]), sb("ones", [1, 128])
        before = sb("before", [128, 128], bf16)
        ones_b = sb("ones_b", [128, 128], bf16)
        iota_e = sb("iota_e", [128, E])
        full = sb("full", [128, GT])
        lower = sb("lower", [128, E, E])
        slotno = sb("slotno", [1, K])
        kwT, owT = sb("kwT", [F, F]), sb("owT", [F, F])
        cols = sb("cols", [F, 4])
        wrT = sb("wrT", [F, E])
        affT, condT = sb("affT", [S, 2, F]), sb("condT", [S, B])
        style, style2, dsum, dtmp, demod = (sb(n, [F, 2, B]) for n in ("style", "style2", "dsum", "dtmp", "demod"))
        w2T = sb("w2T", [128, E, Q, F])
        FB = FF + F
        b12p = sb("b12p", [128, E, FB], bf16)
        xall, zall = sb("xall", [128, B, F]), sb("zall", [128, B, F])
        w01 = sb("w01", [128, B, TOP])
        xT, kT, oT, zT = (sb(n, [F, J, N]) for n in ("xT", "kT", "oT", "zT"))
        kk = sb("kk", [128, 2, J, 2, F])
        prod = sb("prod", [128, J, R, F])
        S2 = sb("S2", [128, J, R, 2, H])
        SF = sb("SF", [128, J, H, H])
        dif = sb("dif", [128, J, H, H])
        prob = sb("prob", [128, 2, J, H, H])
        mx, rs, rinv = sb("mx", [128, J, H]), sb("rs", [128, J, H]), sb("rinv", [128, J, H])
        av = sb("av", [128, J, H, F])
        raw = av[:, :, :, :].rearrange("p j h f -> p (j h f)")
        w1 = raw[:, 0:E * FF].rearrange("p (e q h) -> p e q h", e=E, q=Q)
        w2 = raw[:, E * FF:2 * E * FF].rearrange("p (e f) -> p e f", e=E)
        lg, top, topf = sb("lg", [128, J, E]), sb("top", [128, J, 8]), sb("topf", [128, J, 8])
        topi = sb("topi", [128, J, 8], u32)
        gap, eg, den = sb("gap", [128, J, 1]), sb("eg", [128, J, 1]), sb("den", [128, J, 1])
        pick = sb("pick", [128, GC, TOP, J, E])
        picked = sb("picked", [128, GC, J, E], bf16)
        rank = sb("rank", [128, GC, J, E])
        over = sb("over", [128, E, GT])
        ntile = sb("ntile", [128, E])
        ahead = sb("ahead", [128, E, E])
        first = sb("first", [128, E])
        shift = sb("shift", [128, E])
        at2 = sb("at2", [128, GC, J, E])
        at3 = sb("at3", [128, GC, TOP, J, E])
        posf = sb("posf", [128, GC, TOP, J])
        pos = sb("pos", [128, 2, GC, TOP, J], i32)
        begun = sb("begun", [1, K, E])
        nbeg, sexp = sb("nbeg", [1, K]), sb("sexp", [1, K])
        slot_exp = sb("slot_exp", [1, 2, K], i32)
        big = sb("big", [128, 2 * K * F])
        xg = big[:, 0:K * F].rearrange("p (k f) -> p k f", k=K)
        yb = big[:, K * F:2 * K * F].rearrange("p (k f) -> p k f", k=K)
        w1T = big[:, 0:E * FF].rearrange("p (e f) -> p e f", e=E)
        b12 = big[0:E, E * FF:E * FF + FB]
        b12s = (big[0:E, E * FF + FB:E * FF + FB + 3 * FB // 2].bitcast(bf16)
                .rearrange("e (a f) -> e a f", a=3))
        b12r = prod[0:E, 0, :, :].rearrange("e r f -> e (r f)")
        b12r = [b12r[:, n * FB:(n + 1) * FB] for n in range(1)] + [prod[0:E, 1, 0:FB // F].rearrange("e r f -> e (r f)")]
        xgT = sb("xgT", [F, 2, 128])
        w1b = sb("w1b", [F, NB, FF])
        h = sb("h", [128, 2, Q, 128])
        yg = sb("yg", [128, GC, TOP, J, F])
        zeros = yg[:, :, :, :, :].rearrange("p a b c f -> p (a b c f)")
        acc = sb("acc", [128, J, F])
        stats = sb("stats", [128, J, 6])
        mv = sb("mv", [128, J, 2])
        var, std, y0, y1, nb = (sb(n, [128, J, 1]) for n in ("var", "std", "y0", "y1", "nb"))
        res = sb("res", [128, 2, J, F])
        kw, ow, kwT2, owT2 = (res[:, 0, n] for n in range(4))
        kaw, oaw = res[:, 1, 0, 0:S], res[:, 1, 1, 0:S]

        pX, pO, pZ, pR, pG, pY = (pb(n) for n in ("pX", "pO", "pZ", "pR", "pG", "pY"))
        pH = [pb("pH0"), pb("pH1")]
        pxg, py = pG[:, 0:128], pY[:, 0:F]
        plg = pR[:, 0:J * E].rearrange("p (j e) -> p j e", e=E)
        prank = pR[:, 32:32 + J * E].rearrange("p (j e) -> p j e", e=E)
        pcount = pR[:, 64:64 + E]

        def tiles(p):
            return p[:, :].rearrange("p (j n) -> p j n", j=J)

        names = ["w_in", "bias_in", "b12_stored", "w12_in", "w1_stored", "zero_set", "xs_zeroed", "const0", "const1",
                 "wt_ps", "wt_ready", "b12_split", "style_ps", "style_ready", "dsum_ps", "std_ready", "demod_ready",
                 "wT_ps", "wT_ready",
                 "xT_ps", "xT_ready", "kT_ps", "kT_ready", "k_ps", "kk_ready", "s_ready", "dup_ready", "sf_ready",
                 "dif_ready", "prob_ready", "av_ready", "o_ps", "oT_ready", "z_ps", "zT_ready", "zt_ps", "z_ready",
                 "lg_ps", "gap_ready", "eg_ready", "picked_ready", "rank_ps", "placed", "slots_ready",
                 "scattered", "xg_ps", "xgT_ready", "h_ps", "h_ready", "y_ps", "y_ready", "y_stored",
                 "acc_used", "var_ready", "std2_ready", "norm_ready", "cen_ready", "fin_ready",
                 "dve_chain", "pool_chain"]
        s = {n: sem(n) for n in names}
        x_in = [sem(f"x_in{n}") for n in range(2)]
        xg_in = [sem(f"xg_in{n}") for n in range(len(LOADS))]
        w1b_in = [sem(f"w1b_in{n}") for n in range(NB)]
        gathered = [sem(f"gathered{n}") for n in range(GC)]
        out_done = [sem(f"out_done{n}") for n in range(2)]

        def slots_at(c, p):
            n = (c - GC - 1) * TURN + p - LAG
            g, k = n // (GC * TURN), n % (GC * TURN)
            return [(g, k)] if 0 <= g < G and k < K else []

        TURNS = GC + 1 + GC * G + 1

        def results_at(c):
            g = (c - 2 * GC - 2) // GC
            if c == TURNS - 1:
                g = G - 1
            elif (c - 2 * GC - 2) % GC:
                g = -1
            return [GC * g + a for a in range(GC)] if 0 <= g < G else []

        with nc.Block() as block:
            @block.sync
            def _(sp):
                def load(dst, src, done):
                    sp.dma_start(dst, src).then_inc(done, 16)

                def load_x(c0, c1, done):
                    load(xall[:, c0 * J:c1 * J], x[c0 * J:c1 * J].rearrange("b n f -> n b f"), done)

                load(kw, k_w, s["w_in"])
                load(ow, o_w, s["w_in"])
                load(kaw, k_aff_w, s["w_in"])
                load(oaw, o_aff_w, s["w_in"])
                load(cond_sb[:, :], cond, s["w_in"])
                load(wr[:, :], Wr, s["w_in"])
                for n, v in enumerate((k_aff_b, k_b, o_aff_b, o_b)):
                    load(rows[n:n + 1, :], v.unsqueeze(0), s["w_in"])
                load_x(0, 1, x_in[0])
                load(w1, W1.rearrange("e (q f) h -> f e q h", q=Q), s["w12_in"])
                load(w2, W2.rearrange("e h f -> h e f"), s["w12_in"])
                load_x(1, C, x_in[1])
                load(br_sb[:, :], br.unsqueeze(0), s["bias_in"])
                load(b12[:, 0:FF], b1, s["bias_in"])
                load(b12[:, FF:FF + F], b2, s["bias_in"])
                load(lnw[:, :], ln_w.unsqueeze(0).broadcast_to([128, F]), s["bias_in"])
                load(lnb[:, :], ln_b.unsqueeze(0).broadcast_to([128, F]), s["bias_in"])
                sp.wait_ge(s["zero_set"], 1)
                xz = xs.rearrange("(p r) f -> p (r f)", p=128)
                width = GC * TOP * J * F
                for n in range(0, K * F, width):
                    m = min(width, K * F - n)
                    load(xz[:, n:n + m], zeros[:, 0:m], s["xs_zeroed"])
                sp.wait_ge(s["b12_split"], 1)
                for a in range(3):
                    load(b12p[a:a + 1].rearrange("a e f -> a (e f)"), b12s[:, a], s["b12_stored"])
                sp.wait_ge(s["wT_ready"], 2 * E)
                load(w1s.rearrange("(e h) f -> h e f", h=F), w1T, s["w1_stored"])
                sp.wait_ge(s["w1_stored"], 16)

                for n in range(K * G):
                    g, k = n // K, n % K
                    if k == 0:
                        sp.wait_ge(s["slots_ready"], g + 1)
                    expert = sp.value_load(slot_exp[0:1, g % 2, k:k + 1], min_val=0, max_val=E - 1)
                    if n >= NB:
                        sp.wait_ge(s["h_ps"], n - NB + 1)
                    load(w1b[:, n % NB], w1s[bass.ds(expert * F, F), :], w1b_in[n % NB])
                for u in range(2):
                    sp.wait_ge(out_done[u], 16 * (C // 2))

            @block.gpsimd
            def _(pool):
                P = nc.gpsimd
                P.memset(ident[:, :], 0.0)
                P.memset(before[:, :], 1.0)
                P.memset(ones_b[:, :], 1.0)
                P.memset(ones[:, :], 1.0)
                P.memset(lower[:, :, :], 1.0)
                P.memset(b12p[:, :, :], 0.0)
                P.memset(zeros, 0.0).then_inc(s["zero_set"], 1)
                P.iota(iota_e[:, :], [[1, E]], base=0, channel_multiplier=0, allow_small_or_imprecise_dtypes=True)
                P.iota(full[:, :], [[128, GT]], base=0, channel_multiplier=0, allow_small_or_imprecise_dtypes=True)
                P.iota(slotno[:, :], [[1, K]], base=0, channel_multiplier=0,
                       allow_small_or_imprecise_dtypes=True).then_inc(s["const0"], 1)
                pool.wait_ge(s["const0"], 1)
                P.affine_select(out=ident[:, :], in_=ident[:, :], compare_op=ALU.not_equal, fill=1.0, base=0,
                                pattern=[[-1, 128]], channel_multiplier=1)
                P.affine_select(out=before[:, :], in_=before[:, :], compare_op=ALU.is_gt, fill=0.0, base=0,
                                pattern=[[1, 128]], channel_multiplier=-1)
                P.affine_select(out=lower[:, :, :], in_=lower[:, :, :], compare_op=ALU.is_gt, fill=0.0, base=0,
                                pattern=[[1, E], [-1, E]], channel_multiplier=0).then_inc(s["const1"], 1)
                pool.wait_ge(s["bias_in"], 16 * 5)
                pool.wait_ge(s["xs_zeroed"], 16 * -(-K // (TOP * GT)))
                chain = Chain(pool, s["pool_chain"])

                def scatter(g):
                    pool.wait_ge(s["slots_ready"], g + 1)
                    pool.wait_ge(s["z_ready"], GC * (g + 1))
                    if g:
                        for n in range(len(LOADS)):
                            pool.wait_ge(xg_in[n], 16 * g)
                    for a in range(GC):
                        for t in range(TOP):
                            for j in range(J):
                                index = bass.IndirectOffsetOnAxis(ap=pos[:, g % 2, a, t, j:j + 1], axis=0)
                                P.indirect_dma_start(xs, index, zall[:, (g * GC + a) * J + j, :], None
                                                     ).then_inc(s["scattered"], 16)

                def gather(g, a):
                    if a == 0:
                        pool.wait_ge(s["y_stored"], 16 * len(STORES) * (g + 1))
                    if g:
                        pool.wait_ge(s["acc_used"], GC * (g - 1) + a + 1)
                    for t in range(TOP):
                        for j in range(J):
                            index = bass.IndirectOffsetOnAxis(ap=pos[:, g % 2, a, t, j:j + 1], axis=0)
                            P.indirect_dma_start(yg[:, a, t, j, :], None, ys, index).then_inc(gathered[a], 16)

                def finish(c):
                    u = c % 2
                    pool.wait_ge(s["cen_ready"], c + 1)
                    chain(P.tensor_tensor(out=res[:, u], in0=res[:, u],
                                          in1=lnw[:, :].unsqueeze(1).broadcast_to([128, J, F]), op=ALU.mult))
                    chain(P.tensor_tensor(out=res[:, u], in0=res[:, u],
                                          in1=lnb[:, :].unsqueeze(1).broadcast_to([128, J, F]), op=ALU.add))
                    P.tensor_tensor(out=res[:, u], in0=res[:, u], in1=xall[:, c * J:c * J + J],
                                    op=ALU.add).then_inc(s["fin_ready"], 1)
                    pool.wait_ge(s["fin_ready"], c + 1)
                    pool.dma_start(out[c * J:c * J + J].rearrange("b n f -> n b f"), res[:, u]
                                   ).then_inc(out_done[u], 16)

                for g in range(G):
                    scatter(g)
                    if g:
                        for a in range(GC):
                            gather(g - 1, a)
                        for a in range(GC):
                            finish(GC * (g - 1) + a)
                for a in range(GC):
                    gather(G - 1, a)
                for a in range(GC):
                    finish(GC * (G - 1) + a)

            @block.scalar
            def _(act):
                A = nc.scalar
                act.wait_ge(s["style_ready"], 2)
                A.activation(dtmp[:, :, :], dsum[:, :, :], ACT.Sqrt).then_inc(s["std_ready"], 1)

                def per_batch(c, dst, src, scales, which, bias, done):
                    for j in range(J):
                        b = c * J + j
                        last = A.activation(dst[:, j], src[:, j], ACT.Identity, scale=scales[:, which, b:b + 1],
                                            bias=bias)
                    last.then_inc(done, 1)

                def style_tokens(c):
                    act.wait_ge(s["xT_ps"], c + 1)
                    per_batch(c, xT, tiles(pX), style, 0, 0.0, s["xT_ready"])

                def demod_keys(c):
                    act.wait_ge(s["kT_ps"], c + 1)
                    per_batch(c, kT, tiles(pX), demod, 0, cols[:, 1:2], s["kT_ready"])

                def keys(c):
                    act.wait_ge(s["k_ps"], c + 1)
                    if c >= 2:
                        act.wait_ge(s["av_ready"], (c - 1) * J)
                    A.copy(kk[:, c % 2], tiles(pX).unsqueeze(2).broadcast_to([128, J, 2, F])
                           ).then_inc(s["kk_ready"], 1)

                def mirror(c):
                    act.wait_ge(s["s_ready"], c + 1)
                    A.copy(S2[:, :, 1:R, 1], S2[:, :, 1:R, 0]).then_inc(s["dup_ready"], 1)
                    A.copy(SF[:, :, 0:R], S2[:, :, :, 0])
                    act.wait_ge(s["dup_ready"], c + 1)
                    whole = S2[:, :, :, :, :]
                    for j in range(J):
                        src = bass.AP(tensor=whole.tensor, offset=S2[:, j].offset + (H - R) * 2 * H + R,
                                      ap=[list(whole.ap[0]), [1 - 2 * H, H - R], [1, H]])
                        last = A.copy(SF[:, j, R:H], src)
                    last.then_inc(s["sf_ready"], 1)

                def exponent(c):
                    act.wait_ge(s["dif_ready"], c + 1)
                    A.activation(prob[:, c % 2], dif[:, :, :, :], ACT.Exp, scale=SCALE).then_inc(s["prob_ready"], 1)

                def style_output(c):
                    act.wait_ge(s["o_ps"], J * c + 2 * J)
                    per_batch(c, oT, tiles(pO), style, 1, 0.0, s["oT_ready"])

                def demod_output(c):
                    act.wait_ge(s["z_ps"], c + 1)
                    per_batch(c, zT, tiles(pZ), demod, 1, cols[:, 3:4], s["zT_ready"])

                def outputs(c):
                    act.wait_ge(s["zt_ps"], c + 1)
                    A.copy(zall[:, c * J:c * J + J], tiles(pZ)).then_inc(s["z_ready"], 1)

                def route(c):
                    act.wait_ge(s["gap_ready"], c + 1)
                    A.activation(eg[:, :, :], gap[:, :, :], ACT.Exp).then_inc(s["eg_ready"], 1)

                def load_tokens(g):
                    act.wait_ge(s["scattered"], 16 * TOP * GT * (g + 1))
                    if g == 0:
                        act.wait_ge(s["w1_stored"], 16)
                        act.wait_ge(s["b12_stored"], 48)
                    else:
                        act.wait_ge(s["xg_ps"], K * g)
                    k0 = 0
                    for n, m in enumerate(LOADS):
                        act.dma_start(xg[:, k0:k0 + m], xs.rearrange("(k t) f -> t k f", t=128)[:, k0:k0 + m]
                                      ).then_inc(xg_in[n], 16)
                        k0 += m

                def store_results(g, k):
                    for n in range(len(STORES)):
                        if k + 1 == sum(STORES[:n + 1]):
                            k0 = k + 1 - STORES[n]
                            if g and n == 0:
                                for a in range(GC):
                                    act.wait_ge(gathered[a], 16 * TOP * J * g)
                            act.wait_ge(s["y_ready"], K * g + k + 1)
                            act.dma_start(ys.rearrange("(k t) f -> t k f", t=128)[:, k0:k + 1], yb[:, k0:k + 1]
                                          ).then_inc(s["y_stored"], 16)

                def tokens_in(n):
                    act.wait_ge(s["xg_ps"], n + 1)
                    if n >= 2:
                        act.wait_ge(s["h_ps"], n - 1)
                    A.copy(xgT[:, n % 2], pxg).then_inc(s["xgT_ready"], 1)

                def results_out(n):
                    g, k = n // K, n % K
                    act.wait_ge(s["y_ps"], n + 1)
                    if g and k == 0:
                        act.wait_ge(s["y_stored"], 16 * len(STORES) * g)
                    A.copy(yb[:, k], py).then_inc(s["y_ready"], 1)

                def slot(g, k):
                    n = K * g + k
                    if k == 0:
                        load_tokens(g)
                        tokens_in(n)
                    act.wait_ge(s["h_ps"], n + 1)
                    if n >= 2:
                        act.wait_ge(s["y_ps"], n - 1)
                    A.activation(h[:, n % 2].rearrange("p q t -> p (q t)"), pH[n % 2][:, :], ACT.Gelu
                                 ).then_inc(s["h_ready"], 1)
                    if k + 1 < K:
                        tokens_in(n + 1)
                    if k:
                        results_out(n - 1)
                        store_results(g, k - 1)
                    if k + 1 == K:
                        results_out(n)
                        store_results(g, k)

                def root(c):
                    act.wait_ge(s["var_ready"], c + 1)
                    A.activation(std[:, :, :], var[:, :, :], ACT.Sqrt).then_inc(s["std2_ready"], 1)

                def normalise(c):
                    act.wait_ge(s["norm_ready"], c + 1)
                    if c >= 2:
                        act.wait_ge(out_done[c % 2], 16 * (c // 2))
                    for j in range(J):
                        last = A.activation(res[:, c % 2, j], acc[:, j], ACT.Identity, scale=y1[:, j], bias=nb[:, j])
                    last.then_inc(s["cen_ready"], 1)

                style_tokens(0)
                demod_keys(0)
                keys(0)
                for e in range(E):
                    for n, dst in enumerate((w1T[:, e], w2T[:, e].rearrange("f q h -> f (q h)"))):
                        act.wait_ge(s["wT_ps"], 2 * e + n + 1)
                        A.copy(dst, pH[n][:, :]).then_inc(s["wT_ready"], 1)

                def places(c, a, b):
                    for p in range(a, b):
                        for g, k in slots_at(c, p):
                            slot(g, k)

                for c in range(C):
                    if c + 1 < C:
                        style_tokens(c + 1)
                    places(c, 0, 1)
                    if c + 1 < C:
                        demod_keys(c + 1)
                    places(c, 1, 5)
                    mirror(c)
                    places(c, 5, 7)
                    exponent(c)
                    places(c, 7, 9)
                    if c + 1 < C:
                        keys(c + 1)
                    if c:
                        style_output(c - 1)
                    places(c, 9, 10)
                    if c:
                        demod_output(c - 1)
                    places(c, 10, 11)
                    if c:
                        outputs(c - 1)
                        route(c - 1)
                    places(c, 11, 12)
                    for m in results_at(c):
                        root(m)
                        normalise(m)
                places(C, 0, 4)
                style_output(C - 1)
                demod_output(C - 1)
                outputs(C - 1)
                route(C - 1)
                for c in range(C, TURNS):
                    places(c, 4 if c == C else 0, TURN)
                    for m in results_at(c):
                        root(m)
                        normalise(m)

            @block.vector
            def _(dve):
                V = nc.vector
                link = Chain(dve, s["dve_chain"])
                dve.wait_ge(s["wt_ps"], 1)
                V.tensor_copy(kwT[:, :], pX[:, 0:128])
                V.tensor_copy(owT[:, :], pX[:, 128:256])
                V.tensor_copy(cols[:, :], pX[:, 256:260])
                V.tensor_copy(wrT[:, :], pX[:, 264:264 + E])
                V.tensor_copy(affT[:, :, :], pG[0:S, 0:256].rearrange("s (a f) -> s a f", a=2))
                V.tensor_copy(condT[:, :], pG[0:S, 256:256 + B]).then_inc(s["wt_ready"], 1)
                dve.wait_ge(s["wt_ready"], 1)
                V.tensor_tensor(out=kwT2, in0=kwT[:, :], in1=kwT[:, :], op=ALU.mult)
                V.tensor_tensor(out=owT2, in0=owT[:, :], in1=owT[:, :], op=ALU.mult)
                dve.wait_ge(s["style_ps"], 1)
                V.tensor_tensor(out=style[:, 0], in0=pO[:, 0:B], in1=cols[:, 0:1].broadcast_to([F, B]), op=ALU.add)
                link(V.tensor_tensor(out=style[:, 1], in0=pO[:, B:2 * B], in1=cols[:, 2:3].broadcast_to([F, B]),
                                     op=ALU.add))
                V.tensor_tensor(out=style2[:, :, :], in0=style[:, :, :], in1=style[:, :, :], op=ALU.mult
                                ).then_inc(s["style_ready"], 1)
                dve.wait_ge(s["dsum_ps"], 1)
                V.tensor_scalar(out=dsum[:, :, :], in0=pZ[:, 0:2 * B].rearrange("p (a b) -> p a b", a=2),
                                scalar1=DEMOD_EPS, scalar2=None, op0=ALU.add).then_inc(s["style_ready"], 1)
                dve.wait_ge(s["std_ready"], 1)

                def rsqrt(out_, v, sd, t):
                    link(V.reciprocal(sd, sd))
                    link(V.tensor_tensor(out=t, in0=sd, in1=v, op=ALU.mult))
                    link(V.tensor_tensor(out=t, in0=t, in1=sd, op=ALU.mult))
                    link(V.tensor_scalar(out=t, in0=t, scalar1=-0.5, scalar2=1.5, op0=ALU.mult, op1=ALU.add))
                    return V.tensor_tensor(out=out_, in0=t, in1=sd, op=ALU.mult)

                rsqrt(demod[:, :, :], dsum[:, :, :], dtmp[:, :, :], style2[:, :, :]).then_inc(s["demod_ready"], 1)
                dve.wait_ge(s["bias_in"], 16 * 5)
                link(V.tensor_copy(b12s[:, 0], b12))
                link(V.tensor_tensor(out=b12r[0], in0=b12, in1=b12s[:, 0], op=ALU.subtract))
                link(V.tensor_copy(b12s[:, 1], b12r[0]))
                link(V.tensor_tensor(out=b12r[1], in0=b12r[0], in1=b12s[:, 1], op=ALU.subtract))
                V.tensor_copy(b12s[:, 2], b12r[1]).then_inc(s["b12_split"], 1)
                dve.wait_ge(s["b12_split"], 1)

                def window(half, j0, nj, dist):
                    whole = kk[:, :, :, :, :]
                    return bass.AP(tensor=whole.tensor, offset=kk[:, half, j0].offset,
                                   ap=[list(whole.ap[0]), [2 * F, nj], [D, dist], [1, F]])

                def scores(c):
                    dve.wait_ge(s["kk_ready"], c + 1)
                    link(V.tensor_tensor(out=prod[:, :, :, :], in0=kk[:, c % 2, :, 0:1].broadcast_to([128, J, R, F]),
                                         in1=window(c % 2, 0, J, R), op=ALU.mult))
                    V.tensor_reduce(out=S2[:, :, :, 0],
                                    in_=prod[:, :, :, :].rearrange("p j r (h d) -> p j r h d", d=D), axis=AX.X,
                                    op=ALU.add).then_inc(s["s_ready"], 1)

                def less_max(c):
                    dve.wait_ge(s["sf_ready"], c + 1)
                    link(V.tensor_reduce(out=mx[:, :, :], in_=SF[:, :, :, :].rearrange("p j s h -> p j h s"),
                                         axis=AX.X, op=ALU.max))
                    V.tensor_tensor(out=dif[:, :, :, :], in0=SF[:, :, :, :],
                                    in1=mx[:, :, :].unsqueeze(2).broadcast_to([128, J, H, H]), op=ALU.subtract
                                    ).then_inc(s["dif_ready"], 1)

                def normalise(c):
                    dve.wait_ge(s["prob_ready"], c + 1)
                    p = prob[:, c % 2]
                    link(V.tensor_reduce(out=rs[:, :, :], in_=p.rearrange("p j s h -> p j h s"), axis=AX.X,
                                         op=ALU.add))
                    link(V.reciprocal(rinv[:, :, :], rs[:, :, :]))
                    link(V.tensor_tensor(out=p, in0=p, in1=rinv[:, :, :].unsqueeze(2).broadcast_to([128, J, H, H]),
                                         op=ALU.mult))

                def attend(c, j):
                    dve.wait_ge(s["o_ps"], J * c + j + 1)
                    p = prob[:, c % 2, j].unsqueeze(3).broadcast_to([128, H, H, D])
                    v = window(c % 2, j, 1, H)
                    v = bass.AP(tensor=v.tensor, offset=v.offset, ap=[list(v.ap[0]), [D, H], [D, H], [1, D]])
                    V.tensor_tensor(out=av[:, j].rearrange("p s (h d) -> p s h d", d=D), in0=p, in1=v, op=ALU.mult
                                    ).then_inc(s["av_ready"], 1)

                def choose(c):
                    a = c % GC
                    dve.wait_ge(s["lg_ps"], c + 1)
                    link(V.tensor_copy(lg[:, :, :], plg))
                    for j in range(J):
                        last = V.max(out=top[:, j], in_=lg[:, j])
                    link(last)
                    V.tensor_tensor(out=gap[:, :, :], in0=top[:, :, 1:2], in1=top[:, :, 0:1], op=ALU.subtract
                                    ).then_inc(s["gap_ready"], 1)
                    for j in range(J):
                        last = V.max_index(out=topi[:, j], in_max=top[:, j], in_values=lg[:, j])
                    link(last)
                    link(V.tensor_copy(topf[:, :, :], topi[:, :, :]))
                    bc = [128, J, E]
                    for t in range(TOP):
                        last = V.tensor_tensor(out=pick[:, a, t], in0=topf[:, :, t:t + 1].broadcast_to(bc),
                                               in1=iota_e[:, :].unsqueeze(1).broadcast_to(bc), op=ALU.is_equal)
                    link(last)
                    V.tensor_tensor(out=picked[:, a], in0=pick[:, a, 0], in1=pick[:, a, 1], op=ALU.add
                                    ).then_inc(s["picked_ready"], 1)

                def place(c):
                    g, a = c // GC, c % GC
                    w = w01[:, c * J:c * J + J]
                    dve.wait_ge(s["eg_ready"], c + 1)
                    link(V.tensor_scalar(out=den[:, :, :], in0=eg[:, :, :], scalar1=1.0, scalar2=None, op0=ALU.add))
                    link(V.reciprocal(w[:, :, 0:1], den[:, :, :]))
                    V.tensor_tensor(out=w[:, :, 1:2], in0=eg[:, :, :], in1=w[:, :, 0:1], op=ALU.mult)
                    dve.wait_ge(s["rank_ps"], c + 1)
                    V.tensor_copy(rank[:, a], prank).then_inc(s["placed"], 1)
                    if a < GC - 1:
                        return
                    link(V.tensor_tensor(out=over[:, :, :], in0=pcount.unsqueeze(2).broadcast_to([128, E, GT]),
                                         in1=full[:, :].unsqueeze(1).broadcast_to([128, E, GT]), op=ALU.is_gt))
                    link(V.tensor_reduce(out=ntile[:, :], in_=over[:, :, :], axis=AX.X, op=ALU.add))
                    link(V.tensor_tensor(out=ahead[:, :, :], in0=ntile[:, :].unsqueeze(1).broadcast_to([128, E, E]),
                                         in1=lower[:, :, :], op=ALU.mult))
                    link(V.tensor_reduce(out=first[:, :], in_=ahead[:, :, :], axis=AX.X, op=ALU.add))
                    link(V.tensor_tensor(out=begun[:, :, :], in0=first[0:1, :].unsqueeze(1).broadcast_to([1, K, E]),
                                         in1=slotno[:, :].unsqueeze(2).broadcast_to([1, K, E]), op=ALU.is_le))
                    link(V.tensor_reduce(out=nbeg[:, :], in_=begun[:, :, :], axis=AX.X, op=ALU.add))
                    link(V.tensor_scalar(out=sexp[:, :], in0=nbeg[:, :], scalar1=-1.0, scalar2=None, op0=ALU.add))
                    V.tensor_copy(slot_exp[:, g % 2], sexp[:, :])
                    link(V.tensor_scalar(out=shift[:, :], in0=first[:, :], scalar1=128.0, scalar2=None,
                                         op0=ALU.mult))
                    link(V.tensor_tensor(out=at2[:, :, :, :].rearrange("p a j e -> p (a j) e"),
                                         in0=rank[:, :, :, :].rearrange("p a j e -> p (a j) e"),
                                         in1=shift[:, :].unsqueeze(1).broadcast_to([128, GT, E]), op=ALU.add))
                    for b in range(GC):
                        last = V.tensor_tensor(out=at3[:, b], in0=at2[:, b:b + 1].broadcast_to([128, TOP, J, E]),
                                               in1=pick[:, b], op=ALU.mult)
                    link(last)
                    link(V.tensor_reduce(out=posf[:, :, :, :].rearrange("p a t j -> p (a t j)"),
                                         in_=at3[:, :, :, :, :].rearrange("p a t j e -> p (a t j) e"), axis=AX.X,
                                         op=ALU.add))
                    if g >= 2:
                        for b in range(GC):
                            dve.wait_ge(gathered[b], 16 * TOP * J * (g - 1))
                    V.tensor_copy(pos[:, g % 2], posf[:, :, :, :]).then_inc(s["slots_ready"], 1)

                def combine(c):
                    g, a = c // GC, c % GC
                    dve.wait_ge(gathered[a], 16 * TOP * J * (g + 1))
                    if c:
                        dve.wait_ge(s["cen_ready"], c)
                    for t in range(TOP):
                        for j in range(J):
                            b = c * J + j
                            last = V.scalar_tensor_tensor(out=acc[:, j], in0=yg[:, a, t, j], scalar=w01[:, b, t:t + 1],
                                                          in1=(acc[:, j] if t else zall[:, b]), op0=ALU.mult,
                                                          op1=ALU.add)
                        if t:
                            last.then_inc(s["acc_used"], 1)
                            dve.wait_ge(s["acc_used"], c + 1)
                        else:
                            link(last)
                    for j in range(J):
                        last = V.bn_stats(out=stats[:, j], in_=acc[:, j])
                    link(last)
                    for j in range(J):
                        last = V.bn_aggr(out=mv[:, j], in_=stats[:, j])
                    link(last)
                    V.tensor_scalar(out=var[:, :, :], in0=mv[:, :, 1:2], scalar1=LN_EPS, scalar2=None, op0=ALU.add
                                    ).then_inc(s["var_ready"], 1)
                    dve.wait_ge(s["std2_ready"], c + 1)
                    link(rsqrt(y1[:, :, :], var[:, :, :], std[:, :, :], y0[:, :, :]))
                    V.scalar_tensor_tensor(out=nb[:, :, :], in0=mv[:, :, 0:1], scalar=-1.0, in1=y1[:, :, :],
                                           op0=ALU.mult, op1=ALU.mult).then_inc(s["norm_ready"], 1)

                for c in range(C):
                    scores(c)
                    if c:
                        attend(c - 1, 0)
                        attend(c - 1, 1)
                    less_max(c)
                    if c:
                        attend(c - 1, 2)
                        attend(c - 1, 3)
                    normalise(c)
                    if c:
                        choose(c - 1)
                        place(c - 1)
                    for m in results_at(c):
                        combine(m)
                for j in range(J):
                    attend(C - 1, j)
                choose(C - 1)
                place(C - 1)
                for c in range(C, TURNS):
                    for m in results_at(c):
                        combine(m)

            @block.tensor
            def _(pe):
                PE = nc.tensor

                def transpose(dst, src, n=128):
                    return PE.transpose(dst, src, ident[0:n, 0:n])

                pe.wait_ge(s["const1"], 1)
                pe.wait_ge(s["w_in"], 16 * 10)
                transpose(pX[:, 0:128], kw)
                transpose(pX[:, 128:256], ow)
                transpose(pX[:, 256:260], rows[:, :], 4)
                transpose(pX[:, 264:264 + E], wr[:, :], E)
                transpose(pG[0:S, 0:128], kaw)
                transpose(pG[0:S, 128:256], oaw)
                transpose(pG[0:S, 256:256 + B], cond_sb[:, :], B).then_inc(s["wt_ps"], 1)
                pe.wait_ge(s["wt_ready"], 1)
                PE.matmul(pO[:, 0:B], affT[:, 0], condT[:, :], start=True, stop=True)
                PE.matmul(pO[:, B:2 * B], affT[:, 1], condT[:, :], start=True, stop=True).then_inc(s["style_ps"], 1)
                pe.wait_ge(s["style_ready"], 1)
                PE.matmul(pZ[:, 0:B], kwT2, style2[:, 0], start=True, stop=True)
                PE.matmul(pZ[:, B:2 * B], owT2, style2[:, 1], start=True, stop=True).then_inc(s["dsum_ps"], 1)
                pe.wait_ge(s["demod_ready"], 1)

                def tokens(c):
                    pe.wait_ge(x_in[min(c, 1)], 16)
                    if c:
                        pe.wait_ge(s["kk_ready"], c)
                    for j in range(J):
                        last = transpose(tiles(pX)[:, j], xall[:, c * J + j])
                    last.then_inc(s["xT_ps"], 1)

                def project(c):
                    pe.wait_ge(s["xT_ready"], c + 1)
                    PE.matmul(pX[:, :], kwT[:, :], xT[:, :, :].rearrange("p j n -> p (j n)"), start=True, stop=True
                              ).then_inc(s["kT_ps"], 1)

                def keys(c):
                    pe.wait_ge(s["kT_ready"], c + 1)
                    for j in range(J):
                        last = transpose(tiles(pX)[:, j], kT[:, j])
                    last.then_inc(s["k_ps"], 1)

                def gather_heads(c):
                    if c:
                        pe.wait_ge(s["oT_ready"], c)
                    for j in range(J):
                        pe.wait_ge(s["av_ready"], J * c + j + 1)
                        for d in range(H):
                            last = PE.matmul(tiles(pO)[:, j], av[:, j, d], ident[:, :], start=d == 0,
                                             stop=d == H - 1, is_transpose=True)
                        last.then_inc(s["o_ps"], 1)

                def project_out(c):
                    pe.wait_ge(s["oT_ready"], c + 1)
                    if c:
                        pe.wait_ge(s["z_ready"], c)
                    PE.matmul(pZ[:, :], owT[:, :], oT[:, :, :].rearrange("p j n -> p (j n)"), start=True, stop=True
                              ).then_inc(s["z_ps"], 1)

                def outputs(c):
                    pe.wait_ge(s["zT_ready"], c + 1)
                    for j in range(J):
                        last = transpose(tiles(pZ)[:, j], zT[:, j])
                    last.then_inc(s["zt_ps"], 1)
                    if c == 0:
                        pe.wait_ge(s["bias_in"], 16 * 5)
                    if c:
                        pe.wait_ge(s["placed"], c)
                    for j in range(J):
                        PE.matmul(plg[:, j], zT[:, j], wrT[:, :], start=True, stop=False)
                        last = PE.matmul(plg[:, j], ones[:, :], br_sb[:, :], start=False, stop=True)
                    last.then_inc(s["lg_ps"], 1)

                def ranks(c):
                    a = c % GC
                    pe.wait_ge(s["picked_ready"], c + 1)
                    if a == 0 and c:
                        pe.wait_ge(s["slots_ready"], c // GC)
                    last = PE.matmul(prank, before[:, :], picked[:, a], start=True, stop=False)
                    for j in range(J - 1):
                        last = PE.matmul(prank[:, j + 1:J], ones_b[:, :],
                                         picked[:, a, j:j + 1].broadcast_to([128, J - 1 - j, E]), start=False,
                                         stop=a == 0 and j == J - 2)
                    for b in range(a):
                        for j in range(J):
                            last = PE.matmul(prank, ones_b[:, :], picked[:, b, j:j + 1].broadcast_to([128, J, E]),
                                             start=False, stop=b == a - 1 and j == J - 1)
                    if a == GC - 1:
                        for n in range(GT):
                            last = PE.matmul(pcount, ones_b[:, :], picked[:, n // J, n % J], start=n == 0,
                                             stop=n == GT - 1)
                    last.then_inc(s["rank_ps"], 1)

                def tokens_in(n):
                    g, k = n // K, n % K
                    pe.wait_ge(xg_in[0 if k < LOADS[0] else 1], 16 * (g + 1))
                    if n:
                        pe.wait_ge(s["xgT_ready"], n)
                    transpose(pxg, xg[:, k]).then_inc(s["xg_ps"], 1)

                expert_of = {}

                def look_up(n):
                    g, k = n // K, n % K
                    expert_of[n] = pe.value_load(slot_exp[0:1, g % 2, k:k + 1], min_val=0, max_val=E - 1)

                def up(n):
                    u, w, expert = n % 2, n % NB, expert_of[n]
                    pe.wait_ge(s["xgT_ready"], n + 1)
                    pe.wait_ge(w1b_in[w], 16 * (n // NB + 1))
                    if n >= 2:
                        pe.wait_ge(s["h_ready"], n - 1)
                    bias = b12p[:, :, :].rearrange("p e f -> p (e f)")
                    for q in range(Q):
                        o = pH[u][:, 128 * q:128 * q + 128]
                        PE.matmul(o, w1b[:, w, 128 * q:128 * q + 128], xgT[:, u], start=True, stop=False)
                        last = PE.matmul(o, bias[:, bass.ds(expert * FB + 128 * q, 128)], ones_b[:, :],
                                         start=False, stop=True)
                    last.then_inc(s["h_ps"], 1)

                def down(n):
                    u, expert = n % 2, expert_of.pop(n)
                    pe.wait_ge(s["h_ready"], n + 1)
                    if n:
                        pe.wait_ge(s["y_ready"], n)
                    w = w2T[:, :, :, :].rearrange("p e q f -> p (e q f)")
                    for q in range(Q):
                        PE.matmul(py, h[:, u, q], w[:, bass.ds(expert * (Q * F) + q * F, F)], start=q == 0, stop=False)
                    bias = b12p[:, :, :].rearrange("p e f -> p (e f)")
                    PE.matmul(py, ones_b[:, :], bias[:, bass.ds(expert * FB + FF, F)], start=False, stop=True
                              ).then_inc(s["y_ps"], 1)

                def slot(g, k):
                    n = K * g + k
                    if k == 0:
                        tokens_in(n)
                        look_up(n)
                    up(n)
                    if k + 1 < K:
                        tokens_in(n + 1)
                        look_up(n + 1)
                    if k:
                        down(n - 1)
                    if k + 1 == K:
                        down(n)

                tokens(0)
                project(0)
                keys(0)
                pe.wait_ge(s["w12_in"], 32)
                pe.wait_ge(s["b12_stored"], 48)
                for e in range(E):
                    if e:
                        pe.wait_ge(s["wT_ready"], 2 * e - 1)
                    for q in range(Q):
                        last = transpose(pH[0][:, 128 * q:128 * q + 128], w1[:, e, q])
                    last.then_inc(s["wT_ps"], 1)
                    if e:
                        pe.wait_ge(s["wT_ready"], 2 * e)
                    for q in range(Q):
                        last = transpose(pH[1][:, 128 * q:128 * q + 128], w2[:, e, 128 * q:128 * q + 128])
                    last.then_inc(s["wT_ps"], 1)
                pe.wait_ge(s["wT_ps"], 2 * E)
                pe.sem_inc(s["o_ps"], J)

                def places(c, a, b):
                    for p in range(a, b):
                        for g, k in slots_at(c, p):
                            slot(g, k)

                for c in range(C):
                    if c + 1 < C:
                        tokens(c + 1)
                    places(c, 0, 1)
                    if c + 1 < C:
                        project(c + 1)
                    places(c, 1, 2)
                    if c + 1 < C:
                        keys(c + 1)
                    places(c, 2, 9)
                    if c:
                        gather_heads(c - 1)
                    places(c, 9, 10)
                    if c:
                        project_out(c - 1)
                    places(c, 10, 11)
                    if c:
                        outputs(c - 1)
                    places(c, 11, 12)
                    if c:
                        ranks(c - 1)
                places(C, 0, 4)
                gather_heads(C - 1)
                project_out(C - 1)
                outputs(C - 1)
                ranks(C - 1)
                places(C, 4, TURN)
                for c in range(C + 1, TURNS):
                    places(c, 0, TURN)


_INS = ['x', 'cond_512', 'L0_cond_k_aff_w', 'L0_cond_k_aff_b', 'L0_cond_k_w', 'L0_cond_k_b', 'L0_cond_o_aff_w',
        'L0_cond_o_aff_b', 'L0_cond_o_w', 'L0_cond_o_b', 'L0_ffn_Wr', 'L0_ffn_br', 'L0_ffn_W1', 'L0_ffn_b1',
        'L0_ffn_W2', 'L0_ffn_b2', 'L0_ffn_ln_w', 'L0_ffn_ln_b']


def kernel(**inputs):
    import numpy as _np
    import concourse.bacc as _bacc
    from concourse import mybir as _mybir
    from concourse.bass_utils import run_bass_kernel_spmd as _run

    nc = _bacc.Bacc("TRN2", target_bir_lowering=False, num_devices=1)
    arrays, args = {}, []
    for name in _INS:
        a = _np.ascontiguousarray(inputs[name])
        arrays[f"in_{name}_dram"] = a
        args.append(nc.dram_tensor(f"in_{name}_dram", a.shape, _mybir.dt.from_np(a.dtype), kind="ExternalInput").ap())
    y = nc.dram_tensor("out_dram", inputs['x'].shape, _mybir.dt.float32, kind="ExternalOutput").ap()
    adaln_ffn(nc, *args, y)
    r = _run(nc, [arrays], core_ids=[0])
    return r.results[0]["out_dram"]
```

```python
import math
from contextlib import ExitStack

import concourse.bass as bass
from concourse import mybir


class Chain:

    def __init__(self, engine, sem):
        self.engine, self.sem, self.n = engine, sem, 0

    def __call__(self, ins):
        self.n += 1
        ins.then_inc(self.sem, 1)
        self.engine.wait_ge(self.sem, self.n)


def adaln_ffn(nc, x, cond, k_aff_w, k_aff_b, k_w, k_b, o_aff_w, o_aff_b, o_w, o_b, Wr, br, W1, b1, W2, b2,
              ln_w, ln_b, out):
    f32, i32, u32, bf16 = mybir.dt.float32, mybir.dt.int32, mybir.dt.uint32, mybir.dt.bfloat16
    ALU, ACT, AX = mybir.AluOpType, mybir.ActivationFunctionType, mybir.AxisListType

    B, N, F = x.shape
    S = cond.shape[1]
    E, FF = W1.shape[0], W1.shape[1]
    Q = FF // 128
    H = 16
    D = F // H
    J = 4
    C = B // J
    R = H // 2 + 1
    GROUPS = (3, 3, 2)
    G, GC = len(GROUPS), max(GROUPS)
    FIRST = [sum(GROUPS[:g]) for g in range(G)]
    TOP = 2
    KS = [TOP * J * n + E - 1 for n in GROUPS]
    K = max(KS)
    SLOT0 = [sum(KS[:g]) for g in range(G)]
    TURN = 10
    LAG = 12
    STORE = 8
    GT = GC * J
    RESULT = 2
    AHEAD = 1
    NX = 8
    NB = 5
    P = 3
    DEMOD_EPS, LN_EPS = 1e-8, 1e-12
    SCALE = 1.0 / math.sqrt(D)

    xs = [nc.dram_tensor(f"xs{p}", (E * GT * 128, F), f32, kind="Internal").ap() for p in range(2)]
    ys = [nc.dram_tensor(f"ys{g}", (KS[g] * 128, F), f32, kind="Internal").ap() for g in range(G)]
    w1s = nc.dram_tensor("w1s", (E * F, FF + Q), f32, kind="Internal").ap()
    b2d = nc.dram_tensor("b2d", (E, P, F), bf16, kind="Internal").ap()

    with ExitStack() as ctx:
        def sb(name, shape, dt=f32):
            return ctx.enter_context(nc.sbuf_tensor(name, shape, dt))

        def pb(name):
            return ctx.enter_context(nc.psum_tensor(name, [128, 512], f32))

        def sem(name):
            return ctx.enter_context(nc.semaphore(name))

        cond_sb, wr = sb("cond_sb", [B, S]), sb("wr", [E, F])
        rows = sb("rows", [4, F])
        br_sb = sb("br_sb", [1, E])
        lnw, lnb = sb("lnw", [128, F]), sb("lnb", [128, F])
        ident, ones = sb("ident", [128, 128]), sb("ones", [1, 128])
        before = sb("before", [128, 128], bf16)
        ones_b = sb("ones_b", [128, 128], bf16)
        iota_e = sb("iota_e", [128, E])
        full = sb("full", [128, GC * J])
        lower = sb("lower", [128, E, E])
        slotno = sb("slotno", [1, K])
        region = sb("region", [128, E])
        kwT, owT = sb("kwT", [F, F]), sb("owT", [F, F])
        cols = sb("cols", [F, 4])
        wrT = sb("wrT", [F, E])
        affT, condT = sb("affT", [S, 2, F]), sb("condT", [S, B])
        style, style2, dsum, dtmp, demod = (sb(n, [F, 2, B]) for n in ("style", "style2", "dsum", "dtmp", "demod"))
        w2T = sb("w2T", [128, E, Q, F])
        b2p = sb("b2p", [32, E, F], bf16)
        xall, zall = sb("xall", [128, B, F]), sb("zall", [128, B, F])
        w01 = sb("w01", [128, B, TOP])
        xT, kT, oT, zT = (sb(n, [F, J, N]) for n in ("xT", "kT", "oT", "zT"))
        kk = sb("kk", [128, 2, J, 2, F])
        prod = sb("prod", [128, J, R, F])
        S2 = sb("S2", [128, J, R, 2, H])
        SF = sb("SF", [128, J, H, H])
        dif = sb("dif", [128, J, H, H])
        prob = sb("prob", [128, 2, J, H, H])
        mx, rs, rinv = sb("mx", [128, J, H]), sb("rs", [128, J, H]), sb("rinv", [128, J, H])
        av = sb("av", [128, J, H, F])
        raw = av[:, :, :, :].rearrange("p j h f -> p (j h f)")
        w1 = raw[:, 0:E * FF].rearrange("p (e q h) -> p e q h", e=E, q=Q)
        w2 = raw[:, E * FF:2 * E * FF].rearrange("p (e f) -> p e f", e=E)
        lg, top, topf = sb("lg", [128, J, E]), sb("top", [128, J, 8]), sb("topf", [128, J, 8])
        topi = sb("topi", [128, J, 8], u32)
        gap, eg, den = sb("gap", [128, 2, J, 1]), sb("eg", [128, 2, J, 1]), sb("den", [128, J, 1])
        pick = sb("pick", [128, GC, TOP, J, E])
        picked = sb("picked", [128, GC, J, E], bf16)
        rank = sb("rank", [128, GC, J, E])
        over = sb("over", [128, E, GC * J])
        taken = sb("taken", [128, E])
        ntile = sb("ntile", [128, E])
        ahead = sb("ahead", [128, E, E])
        first = sb("first", [128, E])
        shift = sb("shift", [128, E])
        at2 = sb("at2", [128, GC, J, E])
        at3 = sb("at3", [128, GC, TOP, J, E])
        posf = sb("posf", [128, GC, TOP, J])
        row_x = sb("row_x", [128, C, TOP, J], i32)
        row_y = sb("row_y", [128, C, TOP, J], i32)
        begun = sb("begun", [1, K, E])
        nbeg, sexp = sb("nbeg", [1, K]), sb("sexp", [1, K])
        opened = sb("opened", [1, K, E])
        open_at, tile_no, tile_x = (sb(n, [1, K]) for n in ("open_at", "tile_no", "tile_x"))
        slot_exp = sb("slot_exp", [1, sum(KS)], i32)
        slot_tile = sb("slot_tile", [1, sum(KS)], i32)
        W1B = FF + Q
        big = sb("big", [128, max((NX + 2 * STORE) * F, E * W1B + FF + F * 9 // 2)])
        xg = big[:, 0:NX * F].rearrange("p (k f) -> p k f", k=NX)
        yb = big[:, NX * F:(NX + 2 * STORE) * F].rearrange("p (u k f) -> p u k f", u=2, k=STORE)
        w1T = big[:, 0:E * W1B].rearrange("p (e f) -> p e f", e=E)
        below = big[0:E, E * W1B:E * W1B + FF + F * 9 // 2]
        b1_sb, b2_sb = below[:, 0:FF], below[:, FF:FF + F]
        b2s = below[:, FF + F:FF + F * 5 // 2].bitcast(bf16).rearrange("e (a f) -> e a f", a=P)
        b2r = [below[:, FF + F * 5 // 2 + n * F:FF + F * 7 // 2 + n * F] for n in range(2)]
        xgT = sb("xgT", [F, 2, 128])
        w1b = sb("w1b", [F, NB, W1B])
        h = sb("h", [128, 2, Q, 128])
        yg = sb("yg", [128, 2, TOP, J, F])
        zeros = yg[:, :, :, :, :].rearrange("p a b c f -> p (a b c f)")
        acc = sb("acc", [128, J, F])
        stats = sb("stats", [128, J, 6])
        mv = sb("mv", [128, J, 2])
        var, y0, y1, nb = (sb(n, [128, J, 1]) for n in ("var", "y0", "y1", "nb"))
        res = sb("res", [128, 2, J, F])
        kw, ow, kwT2, owT2 = (res[:, 0, n] for n in range(4))
        kaw, oaw = res[:, 1, 0, 0:S], res[:, 1, 1, 0:S]

        pX, pO, pZ, pR, pG, pY = (pb(n) for n in ("pX", "pO", "pZ", "pR", "pG", "pY"))
        pH = [pb("pH0"), pb("pH1")]
        pxg, py = pG[:, 0:128], pY[:, 0:F]
        plg = pR[:, 0:J * E].rearrange("p (j e) -> p j e", e=E)
        prank = pR[:, 32:32 + J * E].rearrange("p (j e) -> p j e", e=E)
        pb1 = pR[:, 0:Q * E].rearrange("p (q e) -> p q e", q=Q)
        pcount = pR[:, 64:64 + E]

        def tiles(p):
            return p[:, :].rearrange("p (j n) -> p j n", j=J)

        names = ["w_in", "bias_in", "b2_kept", "b2_placed", "b1_ps", "b1_ready", "w12_in", "w1_stored", "zero_set",
                 "const0", "const1",
                 "wt_ps", "wt_ready", "b2_split", "style_ps", "style_ready", "dsum_ps", "std_ready", "demod_ready",
                 "wT_ps", "wT_ready",
                 "xT_ps", "xT_ready", "kT_ps", "kT_ready", "k_ps", "kk_ready", "s_ready", "dup_ready", "sf_ready",
                 "dif_ready", "prob_ready", "av_ready", "o_ps", "oT_ready", "z_ps", "zT_ready", "zt_ps", "z_ready",
                 "lg_ps", "gap_ready", "eg_ready", "picked_ready", "rank_ps", "placed", "aimed", "slots_ready",
                 "rows_ready",
                 "xg_ps", "xgT_ready", "h_ps", "h_ready", "y_ps", "y_ready",
                 "acc_used", "cen_ready", "x_shifted", "fin_ready",
                 "dve_chain",]
        s = {n: sem(n) for n in names}
        x_in = [sem(f"x_in{n}") for n in range(2)]
        zeroed = [sem(f"zeroed{n}") for n in range(2)]
        scattered = [sem(f"scattered{n}") for n in range(2)]
        xg_in = [sem(f"xg_in{n}") for n in range(NX)]
        w1b_in = [sem(f"w1b_in{n}") for n in range(NB)]
        y_stored = [sem(f"y_stored{n}") for n in range(2)]
        gathered = [sem(f"gathered{n}") for n in range(2)]
        out_done = [sem(f"out_done{n}") for n in range(2)]
        late_done = [sem(f"late_done{n}") for n in range(2)]

        place0 = []
        for g in range(G):
            after = [place0[-1] + KS[g - 1]] if g else []
            place0.append(max(after + [(FIRST[g] + GROUPS[g]) * TURN + LAG]))
        TURNS = -(-(place0[-1] + KS[-1]) // TURN)

        def slots_at(c, p):
            n = c * TURN + p
            return [(g, n - place0[g]) for g in range(G) if 0 <= n - place0[g] < KS[g]]

        def results_at(c):
            found = []
            for g in range(G):
                for a in range(GROUPS[g]):
                    if c == min((place0[g] + KS[g]) // TURN + RESULT + a, TURNS - 1):
                        found.append(FIRST[g] + a)
            return found

        LATE = range(FIRST[-1], C)

        def chunk_stored(c):
            if c in LATE:
                return late_done[c % 2], 16 * ((c - LATE[0]) // 2 + 1)
            return out_done[c % 2], 16 * (c // 2 + 1)

        def group_of(c):
            g = max(g for g in range(G) if FIRST[g] <= c)
            return g, c - FIRST[g]

        def stores(g):
            return sum(-(-k // STORE) for k in KS[:g + 1])

        with nc.Block() as block:
            @block.sync
            def _(sp):
                def load(dst, src, done):
                    sp.dma_start(dst, src).then_inc(done, 16)

                def load_x(c0, c1, done):
                    load(xall[:, c0 * J:c1 * J], x[c0 * J:c1 * J].rearrange("b n f -> n b f"), done)

                load(kw, k_w, s["w_in"])
                load(ow, o_w, s["w_in"])
                load(kaw, k_aff_w, s["w_in"])
                load(oaw, o_aff_w, s["w_in"])
                load(cond_sb[:, :], cond, s["w_in"])
                load(wr[:, :], Wr, s["w_in"])
                for n, v in enumerate((k_aff_b, k_b, o_aff_b, o_b)):
                    load(rows[n:n + 1, :], v.unsqueeze(0), s["w_in"])
                load(w1, W1.rearrange("e (q f) h -> f e q h", q=Q), s["w12_in"])
                load(w2, W2.rearrange("e h f -> h e f"), s["w12_in"])
                load_x(1, C, x_in[1])
                load(br_sb[:, :], br.unsqueeze(0), s["bias_in"])
                load(b1_sb, b1, s["bias_in"])
                load(b2_sb, b2, s["bias_in"])
                load(lnw[:, :], ln_w.unsqueeze(0).broadcast_to([128, F]), s["bias_in"])
                load(lnb[:, :], ln_b.unsqueeze(0).broadcast_to([128, F]), s["bias_in"])
                sp.wait_ge(s["zero_set"], 1)
                width = 2 * TOP * J * F
                for p in range(2):
                    xz = xs[p].rearrange("(p r) f -> p (r f)", p=128)
                    for n in range(0, E * GT * F, width):
                        load(xz[:, n:n + width], zeros, zeroed[p])
                sp.wait_ge(s["b2_split"], 1)
                load(b2d, b2s, s["b2_kept"])
                sp.wait_ge(s["b2_kept"], 16)
                load(b2p[0:P, :, :], b2d.rearrange("e a f -> a e f"), s["b2_placed"])
                sp.wait_ge(s["b1_ready"], 1)
                sp.wait_ge(s["wT_ready"], 2 * E)
                load(w1s.rearrange("(e h) f -> h e f", h=F), w1T, s["w1_stored"])
                sp.wait_ge(s["w1_stored"], 16)

                
                for g in range(G):
                    sp.wait_ge(s["slots_ready"], g + 1)
                    end = SLOT0[g] + KS[g]

                    def load_slot_tokens(n):
                        tile = sp.value_load(slot_tile[0:1, n:n + 1], min_val=0, max_val=E * GT - 1)
                        if n >= NX:
                            sp.wait_ge(s["xg_ps"], n - NX + 1)
                        if n == SLOT0[g]:
                            sp.wait_ge(scattered[g % 2], 16 * TOP * J * sum(GROUPS[g % 2:g + 1:2]))
                        load(xg[:, n % NX], xs[g % 2][bass.ds(tile * 128, 128), :], xg_in[n % NX])

                    for n in range(SLOT0[g], SLOT0[g] + AHEAD):
                        load_slot_tokens(n)
                    for n in range(SLOT0[g], end):
                        if n + AHEAD < end:
                            load_slot_tokens(n + AHEAD)
                        expert = sp.value_load(slot_exp[0:1, n:n + 1], min_val=0, max_val=E - 1)
                        if n >= NB:
                            sp.wait_ge(s["h_ready"], n - NB + 1)
                        load(w1b[:, n % NB], w1s[bass.ds(expert * F, F), :], w1b_in[n % NB])
                for c in LATE:
                    sp.wait_ge(s["fin_ready"], c + 1)
                    load(out[c * J:c * J + J].rearrange("b n f -> n b f"), res[:, c % 2], late_done[c % 2])
                for c in range(C):
                    sp.wait_ge(*chunk_stored(c))

            @block.gpsimd
            def _(pool):
                GP = nc.gpsimd
                GP.memset(ident[:, :], 0.0)
                GP.memset(before[:, :], 1.0)
                GP.memset(ones_b[:, :], 1.0)
                GP.memset(ones[:, :], 1.0)
                GP.memset(lower[:, :, :], 1.0)
                GP.memset(b2p[:, :, :], 0.0)
                GP.memset(zeros, 0.0).then_inc(s["zero_set"], 1)
                GP.iota(iota_e[:, :], [[1, E]], base=0, channel_multiplier=0, allow_small_or_imprecise_dtypes=True)
                GP.iota(region[:, :], [[GT * 128, E]], base=0, channel_multiplier=0,
                        allow_small_or_imprecise_dtypes=True)
                GP.iota(full[:, :], [[128, GC * J]], base=0, channel_multiplier=0, allow_small_or_imprecise_dtypes=True)
                GP.iota(slotno[:, :], [[1, K]], base=0, channel_multiplier=0,
                       allow_small_or_imprecise_dtypes=True).then_inc(s["const0"], 1)
                pool.wait_ge(s["const0"], 1)
                GP.affine_select(out=ident[:, :], in_=ident[:, :], compare_op=ALU.not_equal, fill=1.0, base=0,
                                pattern=[[-1, 128]], channel_multiplier=1)
                GP.affine_select(out=before[:, :], in_=before[:, :], compare_op=ALU.is_gt, fill=0.0, base=0,
                                pattern=[[1, 128]], channel_multiplier=-1)
                GP.affine_select(out=lower[:, :, :], in_=lower[:, :, :], compare_op=ALU.is_gt, fill=0.0, base=0,
                                pattern=[[1, E], [-1, E]], channel_multiplier=0).then_inc(s["const1"], 1)
                pool.wait_ge(s["bias_in"], 16 * 5)

                def scatter(c):
                    g, a = group_of(c)
                    pool.wait_ge(s["aimed"], c + 1)
                    pool.wait_ge(s["z_ready"], c + 1)
                    if a == 0:
                        pool.wait_ge(zeroed[g % 2], 16 * -(-E * GT // (2 * TOP * J)))
                    if a == 0 and g >= 2:
                        pool.wait_ge(s["xg_ps"], SLOT0[g - 1])
                    for t in range(TOP):
                        for j in range(J):
                            index = bass.IndirectOffsetOnAxis(ap=row_x[:, c, t, j:j + 1], axis=0)
                            GP.indirect_dma_start(xs[g % 2], index, zall[:, c * J + j, :], None
                                                 ).then_inc(scattered[g % 2], 16)

                def gather(c):
                    g, a = group_of(c)
                    if c == 0:
                        pool.wait_ge(zeroed[1], 16 * -(-E * GT // (2 * TOP * J)))
                    if a == 0:
                        pool.wait_ge(s["rows_ready"], g + 1)
                        for u in range(2):
                            pool.wait_ge(y_stored[u], 16 * ((stores(g) + 1 - u) // 2))
                    if c >= 2:
                        pool.wait_ge(s["acc_used"], c - 1)
                    for t in range(TOP):
                        for j in range(J):
                            index = bass.IndirectOffsetOnAxis(ap=row_y[:, c, t, j:j + 1], axis=0)
                            GP.indirect_dma_start(yg[:, c % 2, t, j, :], None, ys[g], index
                                                 ).then_inc(gathered[c % 2], 16)

                def store_out(c):
                    pool.wait_ge(s["fin_ready"], c + 1)
                    pool.dma_start(out[c * J:c * J + J].rearrange("b n f -> n b f"), res[:, c % 2]
                                   ).then_inc(out_done[c % 2], 16)

                def shift_residual(c):
                    pool.wait_ge(s["xT_ps"], c + 1)
                    GP.tensor_tensor(out=xall[:, c * J:c * J + J], in0=xall[:, c * J:c * J + J],
                                     in1=lnb[:, :].unsqueeze(1).broadcast_to([128, J, F]), op=ALU.add
                                     ).then_inc(s["x_shifted"], 1)

                for c in range(TURNS):
                    if 1 <= c <= C:
                        scatter(c - 1)
                        shift_residual(c - 1)
                    for m in results_at(c):
                        gather(m)
                        if m and m - 1 not in LATE:
                            store_out(m - 1)

            @block.scalar
            def _(act):
                A = nc.scalar
                act.dma_start(xall[:, 0:J], x[0:J].rearrange("b n f -> n b f")).then_inc(x_in[0], 16)

                def per_batch(c, dst, src, scales, which, bias, done):
                    for j in range(J):
                        b = c * J + j
                        last = A.activation(dst[:, j], src[:, j], ACT.Identity, scale=scales[:, which, b:b + 1],
                                            bias=bias)
                    last.then_inc(done, 1)

                def style_tokens(c):
                    act.wait_ge(s["xT_ps"], c + 1)
                    per_batch(c, xT, tiles(pX), style, 0, 0.0, s["xT_ready"])

                def demod_keys(c):
                    act.wait_ge(s["kT_ps"], c + 1)
                    per_batch(c, kT, tiles(pX), demod, 0, cols[:, 1:2], s["kT_ready"])

                def keys(c):
                    act.wait_ge(s["k_ps"], c + 1)
                    if c >= 2:
                        act.wait_ge(s["av_ready"], (c - 1) * J)
                    A.copy(kk[:, c % 2], tiles(pX).unsqueeze(2).broadcast_to([128, J, 2, F])
                           ).then_inc(s["kk_ready"], 1)

                def mirror(c):
                    act.wait_ge(s["s_ready"], c + 1)
                    A.copy(S2[:, :, 1:R, 1], S2[:, :, 1:R, 0]).then_inc(s["dup_ready"], 1)
                    A.copy(SF[:, :, 0:R], S2[:, :, :, 0])
                    act.wait_ge(s["dup_ready"], c + 1)
                    whole = S2[:, :, :, :, :]
                    for j in range(J):
                        src = bass.AP(tensor=whole.tensor, offset=S2[:, j].offset + (H - R) * 2 * H + R,
                                      ap=[list(whole.ap[0]), [1 - 2 * H, H - R], [1, H]])
                        last = A.copy(SF[:, j, R:H], src)
                    last.then_inc(s["sf_ready"], 1)

                def exponent(c):
                    act.wait_ge(s["dif_ready"], c + 1)
                    A.activation(prob[:, c % 2], dif[:, :, :, :], ACT.Exp, scale=SCALE).then_inc(s["prob_ready"], 1)

                def style_output(c):
                    act.wait_ge(s["o_ps"], J * c + 2 * J)
                    per_batch(c, oT, tiles(pO), style, 1, 0.0, s["oT_ready"])

                def demod_output(c):
                    act.wait_ge(s["z_ps"], c + 1)
                    per_batch(c, zT, tiles(pZ), demod, 1, cols[:, 3:4], s["zT_ready"])

                def outputs(c):
                    act.wait_ge(s["zt_ps"], c + 1)
                    A.copy(zall[:, c * J:c * J + J], tiles(pZ)).then_inc(s["z_ready"], 1)

                def route(c):
                    act.wait_ge(s["gap_ready"], c + 1)
                    A.activation(eg[:, c % 2], gap[:, c % 2], ACT.Exp).then_inc(s["eg_ready"], 1)

                def store_results(g, k):
                    if (k + 1) % STORE and k + 1 != KS[g]:
                        return
                    k0 = k - k % STORE
                    m = stores(g - 1) + k // STORE
                    act.wait_ge(s["y_ready"], SLOT0[g] + k + 1)
                    act.dma_start(ys[g].rearrange("(k t) f -> t k f", t=128)[:, k0:k + 1],
                                  yb[:, m % 2, 0:k - k0 + 1]).then_inc(y_stored[m % 2], 16)

                def tokens_in(n):
                    act.wait_ge(s["xg_ps"], n + 1)
                    if n >= 2:
                        act.wait_ge(s["h_ps"], n - 1)
                    A.copy(xgT[:, n % 2], pxg).then_inc(s["xgT_ready"], 1)

                def results_out(g, k):
                    n, m = SLOT0[g] + k, stores(g - 1) + k // STORE
                    act.wait_ge(s["y_ps"], n + 1)
                    if m >= 2:
                        act.wait_ge(y_stored[m % 2], 16 * (m // 2))
                    A.copy(yb[:, m % 2, k % STORE], py).then_inc(s["y_ready"], 1)

                def slot(g, k):
                    n = SLOT0[g] + k
                    if k == 0:
                        tokens_in(n)
                    if k + 1 < KS[g]:
                        tokens_in(n + 1)
                    act.wait_ge(s["h_ps"], n + 1)
                    if n >= 2:
                        act.wait_ge(s["y_ps"], n - 1)
                    for q in range(Q):
                        last = A.activation(h[:, n % 2, q], pH[n % 2][:, 128 * q:128 * q + 128], ACT.Gelu,
                                            bias=w1b[:, n % NB, FF + q:FF + q + 1])
                    last.then_inc(s["h_ready"], 1)
                    if k:
                        results_out(g, k - 1)
                        store_results(g, k - 1)
                    if k + 1 == KS[g]:
                        results_out(g, k)
                        store_results(g, k)

                def expert_weights(e):
                    for n, dst in enumerate((w1T[:, e, 0:FF], w2T[:, e].rearrange("f q h -> f (q h)"))):
                        act.wait_ge(s["wT_ps"], 2 * e + n + 1)
                        A.copy(dst, pH[n][:, :]).then_inc(s["wT_ready"], 1)

                act.wait_ge(s["style_ready"], 1)
                style_tokens(0)
                act.wait_ge(s["style_ready"], 2)
                A.activation(dtmp[:, :, :], dsum[:, :, :], ACT.Sqrt).then_inc(s["std_ready"], 1)
                expert_weights(0)
                act.wait_ge(s["demod_ready"], 1)
                demod_keys(0)
                expert_weights(1)
                keys(0)
                for e in range(2, E):
                    expert_weights(e)

                def places(c, a, b):
                    for p in range(a * TURN // 12, b * TURN // 12):
                        for g, k in slots_at(c, p):
                            slot(g, k)

                for c in range(C):
                    if c + 1 < C:
                        style_tokens(c + 1)
                    places(c, 0, 1)
                    if c + 1 < C:
                        demod_keys(c + 1)
                    places(c, 1, 3)
                    if c:
                        style_output(c - 1)
                    places(c, 3, 4)
                    if c:
                        demod_output(c - 1)
                    places(c, 4, 5)
                    if c:
                        outputs(c - 1)
                    mirror(c)
                    places(c, 5, 8)
                    exponent(c)
                    if c:
                        route(c - 1)
                    places(c, 8, 10)
                    if c + 1 < C:
                        keys(c + 1)
                    places(c, 10, 12)
                places(C, 0, 2)
                style_output(C - 1)
                demod_output(C - 1)
                outputs(C - 1)
                places(C, 2, 4)
                route(C - 1)
                places(C, 4, 12)
                for c in range(C + 1, TURNS):
                    places(c, 0, 12)

            @block.vector
            def _(dve):
                V = nc.vector
                link = Chain(dve, s["dve_chain"])
                dve.wait_ge(s["wt_ps"], 1)
                V.tensor_copy(kwT[:, :], pX[:, 0:128])
                V.tensor_copy(owT[:, :], pX[:, 128:256])
                V.tensor_copy(cols[:, :], pX[:, 256:260])
                V.tensor_copy(wrT[:, :], pX[:, 264:264 + E])
                V.tensor_copy(affT[:, :, :], pG[0:S, 0:256].rearrange("s (a f) -> s a f", a=2))
                V.tensor_copy(condT[:, :], pG[0:S, 256:256 + B]).then_inc(s["wt_ready"], 1)
                dve.wait_ge(s["wt_ready"], 1)
                V.tensor_tensor(out=kwT2, in0=kwT[:, :], in1=kwT[:, :], op=ALU.mult)
                V.tensor_tensor(out=owT2, in0=owT[:, :], in1=owT[:, :], op=ALU.mult)
                dve.wait_ge(s["style_ps"], 1)
                V.tensor_tensor(out=style[:, 0], in0=pO[:, 0:B], in1=cols[:, 0:1].broadcast_to([F, B]), op=ALU.add)
                link(V.tensor_tensor(out=style[:, 1], in0=pO[:, B:2 * B], in1=cols[:, 2:3].broadcast_to([F, B]),
                                     op=ALU.add))
                V.tensor_tensor(out=style2[:, :, :], in0=style[:, :, :], in1=style[:, :, :], op=ALU.mult
                                ).then_inc(s["style_ready"], 1)
                dve.wait_ge(s["dsum_ps"], 1)
                V.tensor_scalar(out=dsum[:, :, :], in0=pZ[:, 0:2 * B].rearrange("p (a b) -> p a b", a=2),
                                scalar1=DEMOD_EPS, scalar2=None, op0=ALU.add).then_inc(s["style_ready"], 1)
                dve.wait_ge(s["std_ready"], 1)

                def rsqrt(out_, v, sd, t):
                    link(V.reciprocal(sd, sd))
                    link(V.tensor_tensor(out=t, in0=sd, in1=v, op=ALU.mult))
                    link(V.tensor_tensor(out=t, in0=t, in1=sd, op=ALU.mult))
                    link(V.tensor_scalar(out=t, in0=t, scalar1=-0.5, scalar2=1.5, op0=ALU.mult, op1=ALU.add))
                    return V.tensor_tensor(out=out_, in0=t, in1=sd, op=ALU.mult)

                rsqrt(demod[:, :, :], dsum[:, :, :], dtmp[:, :, :], style2[:, :, :]).then_inc(s["demod_ready"], 1)
                def window(half, j0, nj, dist):
                    whole = kk[:, :, :, :, :]
                    return bass.AP(tensor=whole.tensor, offset=kk[:, half, j0].offset,
                                   ap=[list(whole.ap[0]), [2 * F, nj], [D, dist], [1, F]])

                def scores(c):
                    dve.wait_ge(s["kk_ready"], c + 1)
                    link(V.tensor_tensor(out=prod[:, :, :, :], in0=kk[:, c % 2, :, 0:1].broadcast_to([128, J, R, F]),
                                         in1=window(c % 2, 0, J, R), op=ALU.mult))
                    V.tensor_reduce(out=S2[:, :, :, 0],
                                    in_=prod[:, :, :, :].rearrange("p j r (h d) -> p j r h d", d=D), axis=AX.X,
                                    op=ALU.add).then_inc(s["s_ready"], 1)

                def split_biases():
                    dve.wait_ge(s["bias_in"], 16 * 5)
                    link(V.tensor_copy(b2s[:, 0], b2_sb))
                    link(V.tensor_tensor(out=b2r[0], in0=b2_sb, in1=b2s[:, 0], op=ALU.subtract))
                    link(V.tensor_copy(b2s[:, 1], b2r[0]))
                    link(V.tensor_tensor(out=b2r[1], in0=b2r[0], in1=b2s[:, 1], op=ALU.subtract))
                    V.tensor_copy(b2s[:, 2], b2r[1]).then_inc(s["b2_split"], 1)
                    dve.wait_ge(s["b1_ps"], 1)
                    for q in range(Q):
                        last = V.tensor_copy(w1T[:, :, FF + q], pb1[:, q])
                    last.then_inc(s["b1_ready"], 1)

                def less_max(c):
                    dve.wait_ge(s["sf_ready"], c + 1)
                    link(V.tensor_reduce(out=mx[:, :, :], in_=SF[:, :, :, :].rearrange("p j s h -> p j h s"),
                                         axis=AX.X, op=ALU.max))
                    V.tensor_tensor(out=dif[:, :, :, :], in0=SF[:, :, :, :],
                                    in1=mx[:, :, :].unsqueeze(2).broadcast_to([128, J, H, H]), op=ALU.subtract
                                    ).then_inc(s["dif_ready"], 1)

                def normalise(c):
                    dve.wait_ge(s["prob_ready"], c + 1)
                    p = prob[:, c % 2]
                    link(V.tensor_reduce(out=rs[:, :, :], in_=p.rearrange("p j s h -> p j h s"), axis=AX.X,
                                         op=ALU.add))
                    link(V.reciprocal(rinv[:, :, :], rs[:, :, :]))
                    link(V.tensor_tensor(out=p, in0=p, in1=rinv[:, :, :].unsqueeze(2).broadcast_to([128, J, H, H]),
                                         op=ALU.mult))

                def attend(c, j):
                    dve.wait_ge(s["o_ps"], J * c + j + 1)
                    p = prob[:, c % 2, j].unsqueeze(3).broadcast_to([128, H, H, D])
                    v = window(c % 2, j, 1, H)
                    v = bass.AP(tensor=v.tensor, offset=v.offset, ap=[list(v.ap[0]), [D, H], [D, H], [1, D]])
                    V.tensor_tensor(out=av[:, j].rearrange("p s (h d) -> p s h d", d=D), in0=p, in1=v, op=ALU.mult
                                    ).then_inc(s["av_ready"], 1)

                def choose(c):
                    a = group_of(c)[1]
                    dve.wait_ge(s["lg_ps"], c + 1)
                    link(V.tensor_copy(lg[:, :, :], plg))
                    for j in range(J):
                        last = V.max(out=top[:, j], in_=lg[:, j])
                    link(last)
                    V.tensor_tensor(out=gap[:, c % 2], in0=top[:, :, 1:2], in1=top[:, :, 0:1], op=ALU.subtract
                                    ).then_inc(s["gap_ready"], 1)
                    for j in range(J):
                        last = V.max_index(out=topi[:, j], in_max=top[:, j], in_values=lg[:, j])
                    link(last)
                    link(V.tensor_copy(topf[:, :, :], topi[:, :, :]))
                    bc = [128, J, E]
                    for t in range(TOP):
                        last = V.tensor_tensor(out=pick[:, a, t], in0=topf[:, :, t:t + 1].broadcast_to(bc),
                                               in1=iota_e[:, :].unsqueeze(1).broadcast_to(bc), op=ALU.is_equal)
                    link(last)
                    V.tensor_tensor(out=picked[:, a], in0=pick[:, a, 0], in1=pick[:, a, 1], op=ALU.add
                                    ).then_inc(s["picked_ready"], 1)

                def weigh(c):
                    w = w01[:, c * J:c * J + J]
                    dve.wait_ge(s["eg_ready"], c + 1)
                    link(V.tensor_scalar(out=den[:, :, :], in0=eg[:, c % 2], scalar1=1.0, scalar2=None, op0=ALU.add))
                    link(V.reciprocal(w[:, :, 0:1], den[:, :, :]))
                    V.tensor_tensor(out=w[:, :, 1:2], in0=eg[:, c % 2], in1=w[:, :, 0:1], op=ALU.mult)

                def place(c):
                    g, a = group_of(c)
                    dve.wait_ge(s["rank_ps"], c + 1)
                    if a == GROUPS[g] - 1:
                        V.tensor_copy(taken[:, :], pcount)
                    V.tensor_copy(rank[:, a], prank).then_inc(s["placed"], 1)
                    dve.wait_ge(s["placed"], c + 1)
                    link(V.tensor_tensor(out=at2[:, a], in0=rank[:, a],
                                         in1=region[:, :].unsqueeze(1).broadcast_to([128, J, E]), op=ALU.add))
                    link(V.tensor_tensor(out=at3[:, a], in0=at2[:, a:a + 1].broadcast_to([128, TOP, J, E]),
                                         in1=pick[:, a], op=ALU.mult))
                    link(V.tensor_reduce(out=posf[:, a], in_=at3[:, a], axis=AX.X, op=ALU.add))
                    V.tensor_copy(row_x[:, c], posf[:, a]).then_inc(s["aimed"], 1)
                    dve.wait_ge(s["aimed"], c + 1)
                    if a < GROUPS[g] - 1:
                        return
                    m, k = GROUPS[g], KS[g]
                    link(V.tensor_tensor(out=over[:, :, 0:m * J],
                                         in0=taken[:, :].unsqueeze(2).broadcast_to([128, E, m * J]),
                                         in1=full[:, 0:m * J].unsqueeze(1).broadcast_to([128, E, m * J]), op=ALU.is_gt))
                    link(V.tensor_reduce(out=ntile[:, :], in_=over[:, :, 0:m * J], axis=AX.X, op=ALU.add))
                    link(V.tensor_tensor(out=ahead[:, :, :], in0=ntile[:, :].unsqueeze(1).broadcast_to([128, E, E]),
                                         in1=lower[:, :, :], op=ALU.mult))
                    link(V.tensor_reduce(out=first[:, :], in_=ahead[:, :, :], axis=AX.X, op=ALU.add))
                    link(V.tensor_tensor(out=begun[:, 0:k], in0=first[0:1, :].unsqueeze(1).broadcast_to([1, k, E]),
                                         in1=slotno[:, 0:k].unsqueeze(2).broadcast_to([1, k, E]), op=ALU.is_le))
                    link(V.tensor_reduce(out=nbeg[:, 0:k], in_=begun[:, 0:k], axis=AX.X, op=ALU.add))
                    link(V.tensor_scalar(out=sexp[:, 0:k], in0=nbeg[:, 0:k], scalar1=-1.0, scalar2=None, op0=ALU.add))
                    V.tensor_copy(slot_exp[:, SLOT0[g]:SLOT0[g] + k], sexp[:, 0:k])
                    link(V.tensor_tensor(out=opened[:, 0:k], in0=first[0:1, :].unsqueeze(1).broadcast_to([1, k, E]),
                                         in1=begun[:, 0:k], op=ALU.mult))
                    link(V.tensor_reduce(out=open_at[:, 0:k], in_=opened[:, 0:k], axis=AX.X, op=ALU.max))
                    link(V.tensor_tensor(out=tile_no[:, 0:k], in0=slotno[:, 0:k], in1=open_at[:, 0:k],
                                         op=ALU.subtract))
                    link(V.tensor_scalar(out=tile_no[:, 0:k], in0=tile_no[:, 0:k], scalar1=GT - 1.0, scalar2=None,
                                         op0=ALU.min))
                    link(V.scalar_tensor_tensor(out=tile_x[:, 0:k], in0=sexp[:, 0:k], scalar=float(GT),
                                                in1=tile_no[:, 0:k], op0=ALU.mult, op1=ALU.add))
                    V.tensor_copy(slot_tile[:, SLOT0[g]:SLOT0[g] + k], tile_x[:, 0:k]).then_inc(s["slots_ready"], 1)
                    link(V.tensor_scalar(out=shift[:, :], in0=first[:, :], scalar1=128.0, scalar2=None,
                                         op0=ALU.mult))
                    link(V.tensor_tensor(out=at2[:, 0:m].rearrange("p a j e -> p (a j) e"),
                                         in0=rank[:, 0:m].rearrange("p a j e -> p (a j) e"),
                                         in1=shift[:, :].unsqueeze(1).broadcast_to([128, m * J, E]), op=ALU.add))
                    for b in range(m):
                        last = V.tensor_tensor(out=at3[:, b], in0=at2[:, b:b + 1].broadcast_to([128, TOP, J, E]),
                                               in1=pick[:, b], op=ALU.mult)
                    link(last)
                    link(V.tensor_reduce(out=posf[:, 0:m].rearrange("p a t j -> p (a t j)"),
                                         in_=at3[:, 0:m].rearrange("p a t j e -> p (a t j) e"), axis=AX.X,
                                         op=ALU.add))
                    V.tensor_copy(row_y[:, FIRST[g]:FIRST[g] + m], posf[:, 0:m]).then_inc(s["rows_ready"], 1)

                def combine(c):
                    a = c % 2
                    dve.wait_ge(gathered[a], 16 * TOP * J * (c // 2 + 1))
                    if c:
                        dve.wait_ge(s["cen_ready"], c)
                    for t in range(TOP):
                        for j in range(J):
                            b = c * J + j
                            last = V.scalar_tensor_tensor(out=acc[:, j], in0=yg[:, a, t, j], scalar=w01[:, b, t:t + 1],
                                                          in1=(acc[:, j] if t else zall[:, b]), op0=ALU.mult,
                                                          op1=ALU.add)
                        if t:
                            last.then_inc(s["acc_used"], 1)
                            dve.wait_ge(s["acc_used"], c + 1)
                        else:
                            link(last)
                    for j in range(J):
                        last = V.bn_stats(out=stats[:, j], in_=acc[:, j])
                    link(last)
                    for j in range(J):
                        last = V.bn_aggr(out=mv[:, j], in_=stats[:, j])
                    link(last)
                    link(V.tensor_scalar(out=var[:, :, :], in0=mv[:, :, 1:2], scalar1=LN_EPS, scalar2=None,
                                         op0=ALU.add))
                    link(V.tensor_scalar(out=y1[:, :, :].bitcast(i32), in0=var[:, :, :].bitcast(i32), scalar1=-0.5,
                                         scalar2=float(0x5F3759DF), op0=ALU.mult, op1=ALU.add))
                    for _ in range(3):
                        link(V.scalar_tensor_tensor(out=y0[:, :, :], in0=y1[:, :, :], scalar=-0.5, in1=y1[:, :, :],
                                                    op0=ALU.mult, op1=ALU.mult))
                        link(V.tensor_tensor(out=y0[:, :, :], in0=y0[:, :, :], in1=var[:, :, :], op=ALU.mult))
                        link(V.scalar_tensor_tensor(out=y1[:, :, :], in0=y0[:, :, :], scalar=1.5, in1=y1[:, :, :],
                                                    op0=ALU.add, op1=ALU.mult))
                    link(V.tensor_scalar(out=nb[:, :, :], in0=mv[:, :, 0:1], scalar1=-1.0, scalar2=None, op0=ALU.mult))
                    u = c % 2
                    if c >= 2:
                        dve.wait_ge(*chunk_stored(c - 2))
                    for j in range(J):
                        last = V.scalar_tensor_tensor(out=res[:, u, j], in0=acc[:, j], scalar=nb[:, j], in1=lnw[:, :],
                                                      op0=ALU.add, op1=ALU.mult)
                    last.then_inc(s["cen_ready"], 1)
                    dve.wait_ge(s["cen_ready"], c + 1)
                    dve.wait_ge(s["x_shifted"], c + 1)
                    for j in range(J):
                        last = V.scalar_tensor_tensor(out=res[:, u, j], in0=res[:, u, j], scalar=y1[:, j],
                                                      in1=xall[:, c * J + j], op0=ALU.mult, op1=ALU.add)
                    last.then_inc(s["fin_ready"], 1)

                for c in range(C):
                    if c:
                        for j in range(J):
                            attend(c - 1, j)
                    scores(c)
                    if c == 0:
                        split_biases()
                    if c:
                        choose(c - 1)
                    less_max(c)
                    if c:
                        place(c - 1)
                    normalise(c)
                    if c:
                        weigh(c - 1)
                    for m in results_at(c):
                        combine(m)
                for j in range(J):
                    attend(C - 1, j)
                choose(C - 1)
                place(C - 1)
                weigh(C - 1)
                for c in range(C, TURNS):
                    for m in results_at(c):
                        combine(m)

            @block.tensor
            def _(pe):
                PE = nc.tensor

                def transpose(dst, src, n=128):
                    return PE.transpose(dst, src, ident[0:n, 0:n])

                pe.wait_ge(s["const1"], 1)
                pe.wait_ge(s["w_in"], 16 * 10)
                transpose(pX[:, 0:128], kw)
                transpose(pX[:, 128:256], ow)
                transpose(pX[:, 256:260], rows[:, :], 4)
                transpose(pX[:, 264:264 + E], wr[:, :], E)
                transpose(pG[0:S, 0:128], kaw)
                transpose(pG[0:S, 128:256], oaw)
                transpose(pG[0:S, 256:256 + B], cond_sb[:, :], B).then_inc(s["wt_ps"], 1)
                pe.wait_ge(s["wt_ready"], 1)
                PE.matmul(pO[:, 0:B], affT[:, 0], condT[:, :], start=True, stop=True)
                PE.matmul(pO[:, B:2 * B], affT[:, 1], condT[:, :], start=True, stop=True).then_inc(s["style_ps"], 1)
                def tokens(c):
                    pe.wait_ge(x_in[min(c, 1)], 16)
                    if c:
                        pe.wait_ge(s["kk_ready"], c)
                    for j in range(J):
                        last = transpose(tiles(pX)[:, j], xall[:, c * J + j])
                    last.then_inc(s["xT_ps"], 1)

                def project(c):
                    pe.wait_ge(s["xT_ready"], c + 1)
                    PE.matmul(pX[:, :], kwT[:, :], xT[:, :, :].rearrange("p j n -> p (j n)"), start=True, stop=True
                              ).then_inc(s["kT_ps"], 1)

                def keys(c):
                    pe.wait_ge(s["kT_ready"], c + 1)
                    for j in range(J):
                        last = transpose(tiles(pX)[:, j], kT[:, j])
                    last.then_inc(s["k_ps"], 1)

                def gather_heads(c):
                    if c:
                        pe.wait_ge(s["oT_ready"], c)
                    for j in range(J):
                        pe.wait_ge(s["av_ready"], J * c + j + 1)
                        for d in range(H):
                            last = PE.matmul(tiles(pO)[:, j], av[:, j, d], ident[:, :], start=d == 0,
                                             stop=d == H - 1, is_transpose=True)
                        last.then_inc(s["o_ps"], 1)

                def project_out(c):
                    pe.wait_ge(s["oT_ready"], c + 1)
                    if c:
                        pe.wait_ge(s["z_ready"], c)
                    PE.matmul(pZ[:, :], owT[:, :], oT[:, :, :].rearrange("p j n -> p (j n)"), start=True, stop=True
                              ).then_inc(s["z_ps"], 1)

                def outputs(c):
                    pe.wait_ge(s["zT_ready"], c + 1)
                    if c == 0:
                        pe.wait_ge(s["bias_in"], 16 * 5)
                    if c:
                        pe.wait_ge(s["placed"], c)
                    for j in range(J):
                        PE.matmul(plg[:, j], zT[:, j], wrT[:, :], start=True, stop=False)
                        last = PE.matmul(plg[:, j], ones[:, :], br_sb[:, :], start=False, stop=True)
                    last.then_inc(s["lg_ps"], 1)
                    for j in range(J):
                        last = transpose(tiles(pZ)[:, j], zT[:, j])
                    last.then_inc(s["zt_ps"], 1)

                def ranks(c):
                    g, a = group_of(c)
                    pe.wait_ge(s["picked_ready"], c + 1)
                    last = PE.matmul(prank, before[:, :], picked[:, a], start=True, stop=False)
                    for j in range(J - 1):
                        last = PE.matmul(prank[:, j + 1:J], ones_b[:, :],
                                         picked[:, a, j:j + 1].broadcast_to([128, J - 1 - j, E]), start=False,
                                         stop=a == 0 and j == J - 2)
                    for b in range(a):
                        for j in range(J):
                            last = PE.matmul(prank, ones_b[:, :], picked[:, b, j:j + 1].broadcast_to([128, J, E]),
                                             start=False, stop=b == a - 1 and j == J - 1)
                    if a == GROUPS[g] - 1:
                        for n in range(GROUPS[g] * J):
                            last = PE.matmul(pcount, ones_b[:, :], picked[:, n // J, n % J], start=n == 0,
                                             stop=n == GROUPS[g] * J - 1)
                    last.then_inc(s["rank_ps"], 1)

                def tokens_in(g, k):
                    n = SLOT0[g] + k
                    pe.wait_ge(xg_in[n % NX], 16 * (n // NX + 1))
                    if n:
                        pe.wait_ge(s["xgT_ready"], n)
                    transpose(pxg, xg[:, n % NX]).then_inc(s["xg_ps"], 1)

                expert_of = {}

                def look_up(n):
                    expert_of[n] = pe.value_load(slot_exp[0:1, n:n + 1], min_val=0, max_val=E - 1)

                def up(n):
                    u, w, expert = n % 2, n % NB, expert_of[n]
                    pe.wait_ge(s["xgT_ready"], n + 1)
                    pe.wait_ge(w1b_in[w], 16 * (n // NB + 1))
                    if n >= 2:
                        pe.wait_ge(s["h_ready"], n - 1)
                    for q in range(Q):
                        last = PE.matmul(pH[u][:, 128 * q:128 * q + 128], w1b[:, w, 128 * q:128 * q + 128],
                                         xgT[:, u], start=True, stop=True)
                    last.then_inc(s["h_ps"], 1)

                def down(n):
                    u, expert = n % 2, expert_of.pop(n)
                    pe.wait_ge(s["h_ready"], n + 1)
                    if n:
                        pe.wait_ge(s["y_ready"], n)
                    w = w2T[:, :, :, :].rearrange("p e q f -> p (e q f)")
                    for q in range(Q):
                        PE.matmul(py, h[:, u, q], w[:, bass.ds(expert * (Q * F) + q * F, F)], start=q == 0, stop=False)
                    bias = b2p[:, :, :].rearrange("p e f -> p (e f)")
                    PE.matmul(py, ones_b[0:32, :], bias[:, bass.ds(expert * F, F)], start=False, stop=True
                              ).then_inc(s["y_ps"], 1)

                def slot(g, k):
                    n = SLOT0[g] + k
                    if k == 0:
                        if g == 0:
                            pe.wait_ge(s["b2_placed"], 16)
                        tokens_in(g, k)
                        look_up(n)
                    if k + 1 < KS[g]:
                        tokens_in(g, k + 1)
                    up(n)
                    if k + 1 < KS[g]:
                        look_up(n + 1)
                    if k:
                        down(n - 1)
                    if k + 1 == KS[g]:
                        down(n)

                def expert_weights(e):
                    if e:
                        pe.wait_ge(s["wT_ready"], 2 * e - 1)
                    for q in range(Q):
                        last = transpose(pH[0][:, 128 * q:128 * q + 128], w1[:, e, q])
                    last.then_inc(s["wT_ps"], 1)
                    if e:
                        pe.wait_ge(s["wT_ready"], 2 * e)
                    for q in range(Q):
                        last = transpose(pH[1][:, 128 * q:128 * q + 128], w2[:, e, 128 * q:128 * q + 128])
                    last.then_inc(s["wT_ps"], 1)

                tokens(0)
                pe.wait_ge(s["style_ready"], 1)
                PE.matmul(pZ[:, 0:B], kwT2, style2[:, 0], start=True, stop=True)
                PE.matmul(pZ[:, B:2 * B], owT2, style2[:, 1], start=True, stop=True).then_inc(s["dsum_ps"], 1)
                pe.wait_ge(s["w12_in"], 32)
                expert_weights(0)
                project(0)
                expert_weights(1)
                keys(0)
                pe.wait_ge(s["bias_in"], 16 * 5)
                for q in range(Q):
                    last = transpose(pb1[:, q], b1_sb[:, 128 * q:128 * q + 128], E)
                last.then_inc(s["b1_ps"], 1)
                for e in range(2, E):
                    expert_weights(e)
                pe.wait_ge(s["wT_ps"], 2 * E)
                pe.sem_inc(s["o_ps"], J)

                def places(c, a, b):
                    for p in range(a * TURN // 12, b * TURN // 12):
                        for g, k in slots_at(c, p):
                            slot(g, k)

                for c in range(C):
                    if c + 1 < C:
                        tokens(c + 1)
                    places(c, 0, 1)
                    if c + 1 < C:
                        project(c + 1)
                    places(c, 1, 3)
                    if c:
                        gather_heads(c - 1)
                    places(c, 3, 4)
                    if c:
                        project_out(c - 1)
                    places(c, 4, 5)
                    if c:
                        outputs(c - 1)
                    places(c, 5, 8)
                    if c:
                        ranks(c - 1)
                    places(c, 8, 10)
                    if c + 1 < C:
                        keys(c + 1)
                    places(c, 10, 12)
                places(C, 0, 2)
                gather_heads(C - 1)
                project_out(C - 1)
                outputs(C - 1)
                places(C, 2, 4)
                ranks(C - 1)
                places(C, 4, 12)
                for c in range(C + 1, TURNS):
                    places(c, 0, 12)


_INS = ['x', 'cond_512', 'L0_cond_k_aff_w', 'L0_cond_k_aff_b', 'L0_cond_k_w', 'L0_cond_k_b', 'L0_cond_o_aff_w',
        'L0_cond_o_aff_b', 'L0_cond_o_w', 'L0_cond_o_b', 'L0_ffn_Wr', 'L0_ffn_br', 'L0_ffn_W1', 'L0_ffn_b1',
        'L0_ffn_W2', 'L0_ffn_b2', 'L0_ffn_ln_w', 'L0_ffn_ln_b']


def kernel(**inputs):
    import numpy as _np
    import concourse.bacc as _bacc
    from concourse import mybir as _mybir
    from concourse.bass_utils import run_bass_kernel_spmd as _run

    nc = _bacc.Bacc("TRN2", target_bir_lowering=False, num_devices=1)
    arrays, args = {}, []
    for name in _INS:
        a = _np.ascontiguousarray(inputs[name])
        arrays[f"in_{name}_dram"] = a
        args.append(nc.dram_tensor(f"in_{name}_dram", a.shape, _mybir.dt.from_np(a.dtype), kind="ExternalInput").ap())
    y = nc.dram_tensor("out_dram", inputs['x'].shape, _mybir.dt.float32, kind="ExternalOutput").ap()
    adaln_ffn(nc, *args, y)
    r = _run(nc, [arrays], core_ids=[0])
    return r.results[0]["out_dram"]
```
